# Optimizing a Trainium2 kernel written in Bass

```python
import numpy as np
import jax
import jax.numpy as jnp

def _softmax(x, axis=-1):
    return jax.nn.softmax(x, axis=axis)

def _gelu(x):
    return jax.nn.gelu(x, approximate=True)

def _silu(x):
    return jax.nn.silu(x)

def _sigmoid(x):
    return jax.nn.sigmoid(x)

def _layernorm(x, axis=-1, eps=1e-05):
    m = jnp.mean(x, axis=axis, keepdims=True)
    v = jnp.var(x, axis=axis, keepdims=True)
    return (x - m) / jnp.sqrt(v + eps)

def _scatter_add(tgt, idx, src, axis=0):
    return tgt.at[idx].add(src)

def _segment_sum(src, seg, n):
    return jax.ops.segment_sum(src, seg, n)
kernel_name = 'mk_perceiver_d1_seqx_r4_75c85e'

def setup_inputs(seed: int=0):
    np.random.seed(seed)
    _w = jnp.asarray

    def _rec_inputs():
        import jax
        import jax.numpy as jnp
        _rk = jax.random.key(seed)
        x = -9.806e-05 + 1 * jax.random.normal(jax.random.fold_in(_rk, 1), (2, 64, 256), jnp.float32)
        _lenS = 64 - jax.random.randint(jax.random.fold_in(_rk, 7), (2,), 0, max(1, 64 // 4) + 1, jnp.int32)
        _lenS2 = 1024 - jax.random.randint(jax.random.fold_in(_rk, 8), (2,), 0, max(1, 1024 // 4) + 1, jnp.int32)
        _ctx_1024P = jax.random.normal(jax.random.fold_in(_rk, 11), (2, 16, 256), jnp.float32)
        _ctx_1024c = jax.random.dirichlet(jax.random.fold_in(_rk, 511), 0.3 * jnp.ones((16,), jnp.float32), (2, 1024))
        _ctx_1024t = jnp.einsum('bsk,bkd->bsd', _ctx_1024c, _ctx_1024P)
        _ctx_1024t = _ctx_1024t * jax.lax.rsqrt(jnp.mean(jnp.square(_ctx_1024t)) + 1e-12) * 0.953939
        ctx_1024 = -1.52775e-05 + 0.999936 * (_ctx_1024t + 0.3 * jax.random.normal(jax.random.fold_in(_rk, 611), (2, 1024, 256), jnp.float32))
        return (x, ctx_1024)
    x, ctx_1024 = _rec_inputs()

    def _L0_xattn_setup():
        import jax, jax.numpy as jnp
        import numpy as np
        D = 256
        NUM_ITERS = 3
        EPS = 1e-06
        SCALE = D ** (-0.5)

        def rmsnorm(x, w, eps=EPS):
            return x * jax.lax.rsqrt(jnp.mean(x * x, axis=-1, keepdims=True) + eps) * w

        def gru_cell(x, h, wih, whh, bih, bhh):
            gx = x @ wih.T + bih
            gh = h @ whh.T + bhh
            xr, xz, xn = jnp.split(gx, 3, axis=-1)
            hr, hz, hn = jnp.split(gh, 3, axis=-1)
            r = jax.nn.sigmoid(xr + hr)
            z = jax.nn.sigmoid(xz + hz)
            n = jnp.tanh(xn + r * hn)
            return (1.0 - z) * n + z * h
        key = jax.random.key(seed)
        ks = jax.random.split(key, 8)
        B, K, M, d = (8, 64, 1024, D)
        w_std = d ** (-0.5)
        return {'slots': jax.random.normal(ks[0], (B, K, d), jnp.float32), 'P': jax.random.normal(ks[1], (B, M, d), jnp.float32), 'Wq': jax.random.normal(ks[2], (d, d), jnp.float32) * w_std, 'Wk': jax.random.normal(ks[3], (d, d), jnp.float32) * w_std, 'Wv': jax.random.normal(ks[4], (d, d), jnp.float32) * w_std, 'gru_wih': jax.random.normal(ks[5], (3 * d, d), jnp.float32) * w_std, 'gru_whh': jax.random.normal(ks[6], (3 * d, d), jnp.float32) * w_std, 'gru_bih': jnp.zeros((3 * d,), jnp.float32), 'gru_bhh': jnp.zeros((3 * d,), jnp.float32), 'slot_norm_w': jnp.ones((d,), jnp.float32), 'input_norm_w': jnp.ones((d,), jnp.float32)}
    _L0_xattn_all = _L0_xattn_setup()
    _L0_xattn_in = {k: v for k, v in _L0_xattn_all.items() if k in ('Wq', 'Wk', 'Wv', 'gru_wih', 'gru_whh', 'gru_bih', 'gru_bhh', 'slot_norm_w', 'input_norm_w')}
    del _L0_xattn_all

    def _L0_attn_setup():
        import jax, jax.numpy as jnp
        import numpy as np
        B, L, D, H = (8, 1024, 256, 16)
        DK = D // H
        key = jax.random.key(seed)
        x = jax.random.normal(key, (B, L, D), dtype=jnp.float32)
        return {'x': x}
    _L0_attn_all = _L0_attn_setup()
    _L0_attn_in = {k: v for k, v in _L0_attn_all.items() if k in ()}
    del _L0_attn_all

    def _L0_ffn_setup():
        import jax, jax.numpy as jnp
        import numpy as np
        B, S, D = (2, 512, 256)
        E, K, DFF = (8, 2, 4 * 256)
        EPS_GATE = 1e-08
        EPS_LN = 1e-05
        key = jax.random.key(seed)
        ks = jax.random.split(key, 4)
        scaled = lambda k, shape, fan: jax.random.normal(k, shape, jnp.float32) / np.sqrt(fan).astype(np.float32)
        return {'x': jax.random.normal(ks[0], (B, S, D), jnp.float32), 'Wg': scaled(ks[1], (D, E), D), 'bg': jnp.zeros((E,), jnp.float32), 'W1': scaled(ks[2], (E, D, DFF), D), 'b1': jnp.zeros((E, DFF), jnp.float32), 'W2': scaled(ks[3], (E, DFF, D), DFF), 'b2': jnp.zeros((E, D), jnp.float32), 'gamma': jnp.ones((D,), jnp.float32), 'beta': jnp.zeros((D,), jnp.float32)}
    _L0_ffn_all = _L0_ffn_setup()
    _L0_ffn_in = {k: v for k, v in _L0_ffn_all.items() if k in ('Wg', 'bg', 'W1', 'b1', 'W2', 'b2', 'gamma', 'beta')}
    del _L0_ffn_all
    return {'x': x, 'ctx_1024': ctx_1024, 'L0_xattn_Wq': _L0_xattn_in['Wq'], 'L0_xattn_Wk': _L0_xattn_in['Wk'], 'L0_xattn_Wv': _L0_xattn_in['Wv'], 'L0_xattn_gru_wih': _L0_xattn_in['gru_wih'], 'L0_xattn_gru_whh': _L0_xattn_in['gru_whh'], 'L0_xattn_gru_bih': _L0_xattn_in['gru_bih'], 'L0_xattn_gru_bhh': _L0_xattn_in['gru_bhh'], 'L0_xattn_slot_norm_w': _L0_xattn_in['slot_norm_w'], 'L0_xattn_input_norm_w': _L0_xattn_in['input_norm_w'], 'L0_ffn_Wg': _L0_ffn_in['Wg'], 'L0_ffn_bg': _L0_ffn_in['bg'], 'L0_ffn_W1': _L0_ffn_in['W1'], 'L0_ffn_b1': _L0_ffn_in['b1'], 'L0_ffn_W2': _L0_ffn_in['W2'], 'L0_ffn_b2': _L0_ffn_in['b2'], 'L0_ffn_gamma': _L0_ffn_in['gamma'], 'L0_ffn_beta': _L0_ffn_in['beta']}

def reference(x, ctx_1024, L0_xattn_Wq, L0_xattn_Wk, L0_xattn_Wv, L0_xattn_gru_wih, L0_xattn_gru_whh, L0_xattn_gru_bih, L0_xattn_gru_bhh, L0_xattn_slot_norm_w, L0_xattn_input_norm_w, L0_ffn_Wg, L0_ffn_bg, L0_ffn_W1, L0_ffn_b1, L0_ffn_W2, L0_ffn_b2, L0_ffn_gamma, L0_ffn_beta):
    import jax
    import jax.numpy as jnp

    def _L0_xattn_ref(slots, P, Wq, Wk, Wv, gru_wih, gru_whh, gru_bih, gru_bhh, slot_norm_w, input_norm_w):
        import jax, jax.numpy as jnp
        import numpy as np
        D = 256
        NUM_ITERS = 3
        EPS = 1e-06
        SCALE = D ** (-0.5)

        def rmsnorm(x, w, eps=EPS):
            return x * jax.lax.rsqrt(jnp.mean(x * x, axis=-1, keepdims=True) + eps) * w

        def gru_cell(x, h, wih, whh, bih, bhh):
            gx = x @ wih.T + bih
            gh = h @ whh.T + bhh
            xr, xz, xn = jnp.split(gx, 3, axis=-1)
            hr, hz, hn = jnp.split(gh, 3, axis=-1)
            r = jax.nn.sigmoid(xr + hr)
            z = jax.nn.sigmoid(xz + hz)
            n = jnp.tanh(xn + r * hn)
            return (1.0 - z) * n + z * h
        Pn = rmsnorm(P, input_norm_w)
        k_proj = Pn @ Wk.T
        v_proj = Pn @ Wv.T
        for _ in range(NUM_ITERS):
            sn = rmsnorm(slots, slot_norm_w)
            q_proj = sn @ Wq.T
            scores = jnp.einsum('bkd,bmd->bkm', q_proj, k_proj) * SCALE
            attn = jax.nn.softmax(scores, axis=-2)
            attn = attn / (jnp.sum(attn, axis=-1, keepdims=True) + EPS)
            updates = jnp.einsum('bkm,bmd->bkd', attn, v_proj)
            slots = gru_cell(updates, slots, gru_wih, gru_whh, gru_bih, gru_bhh)
        return slots

    def _L0_attn_ref(x):
        import jax, jax.numpy as jnp
        import numpy as np
        B, L, D, H = (8, 1024, 256, 16)
        DK = D // H
        Bx, Lx, Dx = x.shape
        xh = x.reshape(Bx, Lx, H, DK).transpose(0, 2, 1, 3)
        m = xh.mean(axis=(0, 1))
        angle = jnp.clip(m @ m.T, -jnp.pi, jnp.pi)
        logits = jnp.sin(angle * 0.5) ** 2
        attn = jax.nn.softmax(logits, axis=-1)
        out = jnp.einsum('ij,bhjd->bhid', attn, xh)
        return out.transpose(0, 2, 1, 3).reshape(Bx, Lx, Dx)

    def _L0_ffn_ref(x, Wg, bg, W1, b1, W2, b2, gamma, beta):
        import jax, jax.numpy as jnp
        import numpy as np
        B, S, D = (2, 512, 256)
        E, K, DFF = (8, 2, 4 * 256)
        EPS_GATE = 1e-08
        EPS_LN = 1e-05
        b, s, d = x.shape
        xf = x.reshape(-1, d)
        T = xf.shape[0]
        num_experts = Wg.shape[1]
        logits = xf @ Wg + bg
        w = jax.nn.softmax(logits, axis=-1)
        top_w, top_idx = jax.lax.top_k(w, K)
        top_w = top_w / (top_w.sum(axis=-1, keepdims=True) + EPS_GATE)
        cw = jnp.zeros((T, num_experts), xf.dtype).at[jnp.arange(T)[:, None], top_idx].add(top_w)
        out = jnp.zeros_like(xf)
        for e in range(num_experts):
            h = jax.nn.gelu(xf @ W1[e] + b1[e], approximate=False)
            y = h @ W2[e] + b2[e]
            out = out + cw[:, e:e + 1] * y
        mu = out.mean(axis=-1, keepdims=True)
        var = out.var(axis=-1, keepdims=True)
        out = (out - mu) / jnp.sqrt(var + EPS_LN) * gamma + beta
        return out.reshape(b, s, d)
    x = x + _L0_xattn_ref(_layernorm(x, axis=-1), ctx_1024, L0_xattn_Wq, L0_xattn_Wk, L0_xattn_Wv, L0_xattn_gru_wih, L0_xattn_gru_whh, L0_xattn_gru_bih, L0_xattn_gru_bhh, L0_xattn_slot_norm_w, L0_xattn_input_norm_w)
    x = x + _L0_attn_ref(_layernorm(x, axis=-1))
    x = x + _L0_ffn_ref(_layernorm(x, axis=-1), L0_ffn_Wg, L0_ffn_bg, L0_ffn_W1, L0_ffn_b1, L0_ffn_W2, L0_ffn_b2, L0_ffn_gamma, L0_ffn_beta)
    return x

_drawn_inputs = setup_inputs


def setup_inputs(seed=0):
    import zlib

    import numpy as np

    out = dict(_drawn_inputs(seed))
    spreads = {'L0_xattn_gru_bih': (0.0, 0.1),
     'L0_xattn_gru_bhh': (0.0, 0.1),
     'L0_xattn_slot_norm_w': (1.0, 0.2),
     'L0_xattn_input_norm_w': (1.0, 0.2),
     'L0_ffn_bg': (0.0, 0.1),
     'L0_ffn_b1': (0.0, 0.1),
     'L0_ffn_b2': (0.0, 0.1),
     'L0_ffn_gamma': (1.0, 0.2),
     'L0_ffn_beta': (0.0, 0.1)}
    factors = {}
    for name, (base, spread) in spreads.items():
        noise = np.random.default_rng([zlib.crc32(name.encode()), seed]).standard_normal(out[name].shape)
        drawn = base * np.exp(spread * noise) if base else spread * noise
        out[name] = jnp.asarray(drawn.astype(out[name].dtype))
    for name, factor in factors.items():
        out[name] = (out[name] * factor).astype(out[name].dtype)
    return out
```

```python
from contextlib import ExitStack

import concourse.bass as bass
from concourse import mybir

F32 = mybir.dt.float32
I32 = mybir.dt.int32
U32 = mybir.dt.uint32
ALU = mybir.AluOpType
ACT = mybir.ActivationFunctionType
AX_X = mybir.AxisListType.X

P = 128
RSQRT_SEED = 1597463007.0
PI = 3.1415927410125732


class Steps:

    def __init__(self, sem):
        self.sem, self.base, self.local, self.turn, self.per_turn = sem, 0, 0, None, 0

    def after(self, instruction):
        instruction.then_inc(self.sem, 1)
        self.local += 1
        return self.local

    def count(self, local):
        if self.turn is None:
            return self.base + local
        return self.turn * self.per_turn + (self.base + local)

    def enter(self, turn, per_turn):
        self.base, self.local, self.turn, self.per_turn = self.base + self.local, 0, turn, per_turn

    def leave(self, turns):
        assert self.local == self.per_turn, (self.local, self.per_turn)
        self.base, self.local, self.turn = self.base + turns * self.per_turn, 0, None


def perceiver_layer(nc, x, ctx, attn_w, gru_w, expert_w, cols, rows, b2, out):
    B, M, D = ctx.shape
    T = x.shape[0]
    K = T // B
    C = D // P
    E = expert_w.shape[0]
    MT = M // P
    FC = (expert_w.shape[2] // (2 * C)) // P
    FF = FC * P
    G = 3 * C
    TURNS = 3
    HEADS = 16
    DK = D // HEADS
    RMS_EPS, SUM_EPS, LN_EPS, GATE_EPS = 1e-6, 1e-6, 1e-5, 1e-8
    SCALE = float(D) ** -0.5
    assert T == P and B == 2 and C == 2

    W_SLOT, W_IN = 0, C
    B_IH = 2 * C
    B_HH = B_IH + G
    B1 = B_HH + G
    WG = B1 + E * FC
    NCOLS = WG + C * E
    R_IN, R_BG, R_GAMMA, R_BETA = 0, D, D + E, 2 * D + E
    NROWS = 3 * D + E
    assert cols.shape[1] == NCOLS and rows.shape[1] == NROWS

    with ExitStack() as stack:
        def sb(name, shape, dt=F32):
            return stack.enter_context(nc.sbuf_tensor(name, shape, dt))

        def sem(name):
            return stack.enter_context(nc.semaphore(name))

        bank = [stack.enter_context(nc.psum_tensor(f"bank{i}", [P, 512], F32)) for i in range(8)]

        def inside(area):
            at = [0]

            def place(shape):
                n = 1
                for k in shape[1:]:
                    n *= k
                assert at[0] + n <= area.shape[1]
                view = area[:, at[0]:at[0] + n]
                at[0] += n
                if len(shape) == 3:
                    view = view.rearrange("p (a b) -> p a b", a=shape[1])
                return view

            return place

        w1w2 = sb("w1w2", [P, E, 2 * C * FF])
        ctx_n = sb("ctx_n", [P, B, MT, D])
        ctx_t = sb("ctx_t", [P, C, B * M])
        aw = sb("aw", [P, 3, C, D])
        gw = sb("gw", [P, 2, C, G * P])
        w_qk = sb("w_qk", [P, C, D])
        w_vi = sb("w_vi", [P, C, G * P])
        colv = sb("colv", [P, NCOLS])
        rowv = sb("rowv", [P, NROWS])
        b2s = sb("b2s", [E, D])
        xs = sb("xs", [P, D])
        xn = sb("xn", [P, D])
        ident = sb("ident", [P, P])
        ones = sb("ones", [P, P])
        same_batch = sb("same_batch", [P, P])
        same_slot = sb("same_slot", [P, P])
        slots = sb("slots", [P, C, T])
        sq = [sb(f"sq{b}", [P, C, K]) for b in range(B)]
        q_t = [sb(f"q_t{b}", [P, C, K]) for b in range(B)]
        attn = [sb(f"attn{b}", [P, MT, K]) for b in range(B)]
        mx = [sb(f"mx{b}", [P, MT]) for b in range(B)]
        den = [sb(f"den{b}", [P, MT]) for b in range(B)]
        u_t = [sb(f"u_t{b}", [P, C, K]) for b in range(B)]
        rs_v = [sb(f"rs_v{b}", [P, K]) for b in range(B)]
        rs_y = [sb(f"rs_y{b}", [P, K]) for b in range(B)]
        rs_a = [sb(f"rs_a{b}", [P, K]) for b in range(B)]
        gru_tile = inside(aw[:, :, :, :].rearrange("p w c d -> p (w c d)"))
        rz = [gru_tile([P, 2 * C, K]) for b in range(B)]
        hh = [gru_tile([P, C, K]) for b in range(B)]
        hq = [gru_tile([P, C, K]) for b in range(B)]
        nn = [gru_tile([P, C, K]) for b in range(B)]
        n2 = [gru_tile([P, C, K]) for b in range(B)]
        b_rz = sb("b_rz", [P, 2 * C])
        b_hn = sb("b_hn", [P, C])
        ms = sb("ms", [P, B, MT])
        ms_v = sb("ms_v", [P, MT])
        ms_y = sb("ms_y", [P, MT])
        ms_a = sb("ms_a", [P, MT])
        r_ctx = sb("r_ctx", [P, B, MT])
        st6 = sb("st6", [P, 6])
        mv = sb("mv", [P, 2])
        s_v = sb("s_v", [P, 1])
        s_y = sb("s_y", [P, 1])
        s_a = sb("s_a", [P, 1])
        rstd = sb("rstd", [P, 1])
        later = inside(ctx_n[:, :, :, :].rearrange("p b t d -> p (b t d)"))

        x1 = later([P, D])
        red = later([P, DK])
        m_t = sb("m_t", [DK, P])
        ang = later([P, P])
        mixw = later([P, P])
        row_sum = sb("row_sum", [P, 1])
        row_inv = sb("row_inv", [P, 1])
        x2 = later([P, D])
        xf_t = later([P, C, T])
        gl = later([P, E])
        g8 = later([P, 8])
        gneg = later([P, 1])
        gsum = later([P, 1])
        ginv = later([P, 1])
        gtop = later([P, 8])
        gix = sb("gix", [P, 8], U32)
        gixf = later([P, 8])
        iota = sb("iota", [P, E])
        pick = later([P, 2, E])
        cw = later([P, E])
        cw_t = sb("cw_t", [E, P])
        h_t = later([P, 4, T])
        acc = later([P, D])
        fin = later([P, D])

        x_in, cols_in, rows_in, b2_in = sem("x_in"), sem("cols_in"), sem("rows_in"), sem("b2_in")
        aw_in, gw_in = sem("aw_in"), sem("gw_in")
        ctx_in = [sem(f"ctx_in{b}") for b in range(B)]
        expert_in = [sem(f"expert_in{e}") for e in range(E)]
        out_done = sem("out_done")
        pool_step, consts_ready = sem("pool_step"), sem("consts_ready")
        vec_step = sem("vec_step")
        ln_ready = sem("ln_ready")
        ctx_sq = sem("ctx_sq")
        r_ready = sem("r_ready")
        ctx_n_act, ctx_n_vec = sem("ctx_n_act"), sem("ctx_n_vec")
        pair_t = sem("pair_t")
        pair_act, pair_vec = sem("pair_act"), sem("pair_vec")
        x_t = sem("x_t")
        w_qk_done, w_vi_done = sem("w_qk_done"), sem("w_vi_done")
        w_out = sem("w_out")
        slots_ready = [sem(f"slots_ready{b}") for b in range(B)]
        sq_ready = [sem(f"sq_ready{b}") for b in range(B)]
        q_raw = [sem(f"q_raw{b}") for b in range(B)]
        gh_ready = [sem(f"gh_ready{b}") for b in range(B)]
        q_ready = [sem(f"q_ready{b}") for b in range(B)]
        scores_ready = [sem(f"scores_ready{b}") for b in range(B)]
        shifted = [sem(f"shifted{b}") for b in range(B)]
        exp_ready = [sem(f"exp_ready{b}") for b in range(B)]
        attn_ready = [sem(f"attn_ready{b}") for b in range(B)]
        u_raw = [sem(f"u_raw{b}") for b in range(B)]
        u_ready = [sem(f"u_ready{b}") for b in range(B)]
        gx_ready = [sem(f"gx_ready{b}") for b in range(B)]
        rz_pre = [sem(f"rz_pre{b}") for b in range(B)]
        rz_ready = [sem(f"rz_ready{b}") for b in range(B)]
        n_pre = [sem(f"n_pre{b}") for b in range(B)]
        n_ready = [sem(f"n_ready{b}") for b in range(B)]
        slots_back = sem("slots_back")
        red_ready, m_raw, m_ready, ang_raw = sem("red_ready"), sem("m_raw"), sem("m_ready"), sem("ang_raw")
        ang_ready, sin_ready, sin2_ready, mix_exp, mix_ready = (
            sem("ang_ready"), sem("sin_ready"), sem("sin2_ready"), sem("mix_exp"), sem("mix_ready"))
        mixed = sem("mixed")
        xf_ready = sem("xf_ready")
        gate_raw, gate_ready, gate_exp, cw_ready, cw_turned, cw_t_ready, bias2 = (
            sem("gate_raw"), sem("gate_ready"), sem("gate_exp"), sem("cw_ready"), sem("cw_turned"),
            sem("cw_t_ready"), sem("bias2"))
        hidden, gelu_done, down_done, y_ready, y_folded = (
            sem("hidden"), sem("gelu_done"), sem("down_done"), sem("y_ready"), sem("y_folded"))
        fin_ready = sem("fin_ready")

        scores = [bank[b][:, :].rearrange("p (t k) -> p t k", t=MT) for b in range(B)]
        gates = [bank[2 + b][:, :].rearrange("p (g k) -> p g k", k=K) for b in range(B)]
        misc = [bank[4 + b] for b in range(B)]
        q_ps = [misc[b][:, 0:C * K].rearrange("p (c k) -> p c k", c=C) for b in range(B)]
        ssq_ps = [misc[b][:, C * K:(C + 1) * K] for b in range(B)]
        u_ps = [misc[b][:, (C + 1) * K:(2 * C + 1) * K].rearrange("p (c k) -> p c k", c=C) for b in range(B)]
        sum_ps = [misc[b][:, (2 * C + 1) * K:(2 * C + 2) * K] for b in range(B)]
        pair_banks = [0, 1, 6]
        PAIRS = B * MT // 2
        HN, XN = 2 * C, 3 * C

        def context_tile(b, t):
            return ctx_n[:, b, t, :].rearrange("p (c m) -> p c m", c=C)

        def squares_at(b, t):
            o = (b * MT + t) * P
            return ctx_t[:, :, o:o + P]

        def pair_act_count(j):
            return j // 2 + 1

        def pair_vec_count(j):
            return (j + 1) // 2

        block = stack.enter_context(nc.Block())

        @block.sync
        def _(sp):
            sp.dma_start(xs[:, :], x[:, :]).then_inc(x_in, 16)
            sp.dma_start(colv[:, :], cols[:, :]).then_inc(cols_in, 16)
            sp.dma_start(ctx_n[:, 0, :, :], ctx[0].rearrange("(p t) d -> p t d", t=MT)).then_inc(ctx_in[0], 16)
            sp.dma_start(aw[:, :, :, :], attn_w[:, :, :, :]).then_inc(aw_in, 16)
            sp.dma_start(rowv[:, :], rows.to_broadcast([P, NROWS])).then_inc(rows_in, 16)
            sp.dma_start(ctx_n[:, 1, :, :], ctx[1].rearrange("(p t) d -> p t d", t=MT)).then_inc(ctx_in[1], 16)
            sp.dma_start(gw[:, :, :, :], gru_w[:, :, :, :]).then_inc(gw_in, 16)
            sp.dma_start(b2s[:, :], b2[:, :]).then_inc(b2_in, 16)
            for e in range(E):
                sp.dma_start(w1w2[:, e, :], expert_w[e]).then_inc(expert_in[e], 16)
            sp.wait_ge(fin_ready, 1)
            sp.dma_start(out[:, :], fin[:, :]).then_inc(out_done, 16)
            sp.wait_ge(out_done, 16)

        @block.gpsimd
        def _(pool):
            def diagonal(m, base):
                return pool.affine_select(out=m[:, :], in_=m[:, :], compare_op=ALU.not_equal, fill=1.0,
                                          base=base, pattern=[[-1, P]], channel_multiplier=1)

            pool.memset(ident[:, :], 0.0).then_inc(pool_step, 1)
            pool.wait_ge(pool_step, 1)
            diagonal(ident, 0).then_inc(consts_ready, 1)
            pool.memset(ones[:, :], 1.0).then_inc(consts_ready, 1)
            pool.memset(same_batch[:, :], 0.0).then_inc(pool_step, 1)
            pool.memset(same_slot[:, :], 0.0).then_inc(pool_step, 1)
            pool.wait_ge(pool_step, 3)
            for b in range(B):
                pool.memset(same_batch[b * K:(b + 1) * K, b * K:(b + 1) * K], 1.0).then_inc(consts_ready, 1)
            pool.wait_ge(consts_ready, 2 + B)
            for i, base in enumerate((0, K, -K)):
                diagonal(same_slot, base).then_inc(pool_step, 1)
                pool.wait_ge(pool_step, 4 + i)
            pool.iota(iota[:, :], pattern=[[1, E]], base=0, channel_multiplier=0,
                      allow_small_or_imprecise_dtypes=True).then_inc(consts_ready, 1)

        CONSTS = 2 + B + 1

        @block.scalar
        def _(act):
            for b in range(B):
                act.wait_ge(ctx_in[b], 16)
                for t in range(1, MT, 2):
                    last = act.activation(squares_at(b, t), context_tile(b, t), ACT.Square,
                                          accum_out=ms[:, b, t:t + 1])
                last.then_inc(ctx_sq, 1)
                act.wait_ge(r_ready, b + 1)
                for t in range(1, MT, 2):
                    act.activation(ctx_n[:, b, t, :], ctx_n[:, b, t, :], ACT.Copy,
                                   scale=r_ctx[:, b, t:t + 1]).then_inc(ctx_n_act, 1)
                for j in range(b * MT // 2, (b + 1) * MT // 2, 2):
                    act.wait_ge(pair_t, j + 1)
                    src = bank[pair_banks[j % 3]][:, :].rearrange("p (c m) -> p c m", c=C)
                    act.activation(ctx_t[:, :, j * 2 * P:(j + 1) * 2 * P], src, ACT.Copy).then_inc(pair_act, 1)

            with act.Fori(0, TURNS) as turn:
                for b in range(B):
                    act.wait_ge(slots_ready[b], turn + 1)
                    act.activation(sq[b][:, :, :], slots[:, :, b * K:(b + 1) * K], ACT.Square)\
                       .then_inc(sq_ready[b], 1)
                for b in range(B):
                    act.wait_ge(shifted[b], turn + 1)
                    act.activation(attn[b][:, :, :], attn[b][:, :, :], ACT.Exp).then_inc(exp_ready[b], 1)
                for b in range(B):
                    act.wait_ge(rz_pre[b], turn + 1)
                    act.activation(rz[b][:, :, :], rz[b][:, :, :], ACT.Tanh, scale=0.5).then_inc(rz_ready[b], 1)
                    act.wait_ge(n_pre[b], turn + 1)
                    act.activation(nn[b][:, :, :], nn[b][:, :, :], ACT.Tanh).then_inc(n_ready[b], 1)

            act.wait_ge(ang_ready, 1)
            act.activation(ang[:, :], ang[:, :], ACT.Sin, scale=0.5).then_inc(sin_ready, 1)
            act.wait_ge(sin2_ready, 1)
            act.activation(mixw[:, :], mixw[:, :], ACT.Exp).then_inc(mix_exp, 1)
            act.wait_ge(gate_ready, 1)
            act.activation(gl[:, :], gl[:, :], ACT.Exp, bias=gneg[:, 0:1], accum_out=gsum[:, 0:1])\
               .then_inc(gate_exp, 1)
            for n in range(E * FC):
                act.wait_ge(hidden, n + 1)
                if n >= 4:
                    act.wait_ge(down_done, n - 3)
                act.activation(h_t[:, n % 4, :], bank[n % 4][:, 0:T], ACT.Gelu,
                               bias=colv[:, B1 + n:B1 + n + 1]).then_inc(gelu_done, 1)

        @block.tensor
        def _(pe):
            pe.wait_ge(consts_ready, 2)
            pe.wait_ge(ln_ready, 1)
            for c in range(C):
                last = pe.transpose(bank[4][:, c * T:(c + 1) * T], xn[:, c * P:(c + 1) * P], ident[:, :])
            last.then_inc(x_t, 1)
            pe.wait_ge(aw_in, 16)
            for i in range(C):
                for c in range(C):
                    last = pe.matmul(bank[7][:, i * D:(i + 1) * D], aw[:, 0, c, i * P:(i + 1) * P],
                                     aw[:, 1, c, :], start=(c == 0), stop=(c == C - 1))
            last.then_inc(w_qk_done, 1)

            def turn_pair(j):
                b, t = divmod(2 * j, MT)
                pe.wait_ge(ctx_n_vec, b * MT // 2 + t // 2 + 1)
                pe.wait_ge(ctx_n_act, b * MT // 2 + t // 2 + 1)
                if j >= 3:
                    if (j - 3) % 2:
                        pe.wait_ge(pair_vec, pair_vec_count(j - 3))
                    else:
                        pe.wait_ge(pair_act, pair_act_count(j - 3))
                for c in range(C):
                    for k in range(2):
                        o = (2 * c + k) * P
                        last = pe.transpose(bank[pair_banks[j % 3]][:, o:o + P],
                                            ctx_n[:, b, t + k, c * P:(c + 1) * P], ident[:, :])
                last.then_inc(pair_t, 1)

            for j in range(PAIRS // 2):
                turn_pair(j)
            pe.wait_ge(gw_in, 16)
            for i in range(C):
                for dst, g0, g1 in ((bank[2 + i][:, :], 0, 2 * C * P),
                                    (bank[5][:, i * C * P:(i + 1) * C * P], 2 * C * P, G * P)):
                    for c in range(C):
                        last = pe.matmul(dst, aw[:, 2, c, i * P:(i + 1) * P], gw[:, 0, c, g0:g1],
                                         start=(c == 0), stop=(c == C - 1))
            last.then_inc(w_vi_done, 1)
            for j in range(PAIRS // 2, PAIRS):
                turn_pair(j)
            pe.wait_ge(w_out, 2)
            pe.wait_ge(pair_act, PAIRS // 2)
            pe.wait_ge(pair_vec, PAIRS // 2)

            def query(b, turn):
                pe.wait_ge(slots_ready[b], turn + 1)
                for i in range(C):
                    for c in range(C):
                        pe.matmul(q_ps[b][:, i, :], w_qk[:, c, i * P:(i + 1) * P],
                                  slots[:, c, b * K:(b + 1) * K], start=(c == 0), stop=(c == C - 1))
                pe.wait_ge(sq_ready[b], turn + 1)
                for c in range(C):
                    last = pe.matmul(ssq_ps[b], ones[:, :], sq[b][:, c, :], start=(c == 0), stop=(c == C - 1))
                last.then_inc(q_raw[b], 1)

            def hidden_gates(b):
                for g in range(G):
                    for c in range(C):
                        last = pe.matmul(gates[b][:, g, :], gw[:, 1, c, g * P:(g + 1) * P],
                                         slots[:, c, b * K:(b + 1) * K],
                                         start=(g == 0 and c == 0), stop=False, skip_group_check=True)
                last.then_inc(gh_ready[b], 1)

            def score(b, turn):
                pe.wait_ge(q_ready[b], turn + 1)
                for t in range(MT):
                    for c in range(C):
                        o = (b * MT + t) * P
                        last = pe.matmul(scores[b][:, t, :], ctx_t[:, c, o:o + P], q_t[b][:, c, :],
                                         start=(c == 0), stop=(c == C - 1))
                last.then_inc(scores_ready[b], 1)

            def update(b, turn):
                pe.wait_ge(attn_ready[b], turn + 1)
                for t in range(MT):
                    pe.matmul(sum_ps[b], ones[:, :], attn[b][:, t, :], start=(t == 0), stop=(t == MT - 1))
                for i in range(C):
                    for t in range(MT):
                        last = pe.matmul(u_ps[b][:, i, :], ctx_n[:, b, t, i * P:(i + 1) * P],
                                         attn[b][:, t, :], start=(t == 0), stop=(t == MT - 1))
                last.then_inc(u_raw[b], 1)

            def input_gates(b, turn):
                pe.wait_ge(u_ready[b], turn + 1)
                for g in range(G):
                    dst = g if g < 2 * C else XN + g - 2 * C
                    for c in range(C):
                        last = pe.matmul(gates[b][:, dst, :], w_vi[:, c, g * P:(g + 1) * P], u_t[b][:, c, :],
                                         start=False, stop=(g == G - 1 and c == C - 1), skip_group_check=True)
                last.then_inc(gx_ready[b], 1)

            with pe.Fori(0, TURNS) as turn:
                query(0, turn)
                hidden_gates(0)
                score(0, turn)
                query(1, turn)
                hidden_gates(1)
                score(1, turn)
                update(0, turn)
                input_gates(0, turn)
                update(1, turn)
                input_gates(1, turn)

            for b in range(B):
                pe.wait_ge(slots_ready[b], TURNS + 1)
            for c in range(C):
                last = pe.transpose(bank[6][:, c * P:(c + 1) * P], slots[:, c, :], ident[:, :])
            last.then_inc(slots_back, 1)
            pe.wait_ge(consts_ready, CONSTS)
            pe.wait_ge(red_ready, 1)
            pe.matmul(bank[7][0:DK, 0:P], red[:, :], same_slot[:, :], start=True, stop=True).then_inc(m_raw, 1)
            pe.wait_ge(m_ready, 1)
            pe.matmul(bank[7][:, P:2 * P], m_t[:, :], m_t[:, :], start=True, stop=True).then_inc(ang_raw, 1)
            pe.wait_ge(mix_ready, 1)
            pe.matmul(bank[6][:, 0:D], mixw[:, :], xn[:, :], start=True, stop=True).then_inc(mixed, 1)
            pe.wait_ge(ln_ready, 3)
            for c in range(C):
                last = pe.transpose(bank[7][:, c * T:(c + 1) * T], xn[:, c * P:(c + 1) * P], ident[:, :])
            last.then_inc(x_t, 1)
            pe.wait_ge(xf_ready, 1)
            for c in range(C):
                last = pe.matmul(bank[6][:, 0:E], xf_t[:, c, :], colv[:, WG + c * E:WG + (c + 1) * E],
                                 start=(c == 0), stop=(c == C - 1))
            last.then_inc(gate_raw, 1)

            def up(n):
                e, f = divmod(n, FC)
                if f == 0:
                    pe.wait_ge(expert_in[e], 16)
                if n >= 4:
                    pe.wait_ge(gelu_done, n - 3)
                for c in range(C):
                    last = pe.matmul(bank[n % 4][:, 0:T], w1w2[:, e, c * FF + f * P:c * FF + (f + 1) * P],
                                     xf_t[:, c, :], start=(c == 0), stop=(c == C - 1))
                last.then_inc(hidden, 1)

            def down(n):
                e, f = divmod(n, FC)
                pe.wait_ge(gelu_done, n + 1)
                if f == 0 and e >= 2:
                    pe.wait_ge(y_folded, e - 1)
                o = C * FF + f * D
                last = pe.matmul(bank[4 + e % 2][:, 0:D], h_t[:, n % 4, :], w1w2[:, e, o:o + D],
                                 start=(f == 0), stop=(f == FC - 1))
                last.then_inc(down_done, 1)

            LAG = 2
            for n in range(E * FC + LAG):
                if n < E * FC:
                    up(n)
                if n >= LAG:
                    down(n - LAG)
                if n == 6:
                    pe.wait_ge(cw_ready, 1)
                    pe.transpose(bank[7][0:E, 256:256 + P], cw[:, :], ident[:, :]).then_inc(cw_turned, 1)
                if n == 8:
                    pe.wait_ge(cw_t_ready, 1)
                    pe.wait_ge(b2_in, 16)
                    pe.matmul(bank[6][:, 256:256 + D], cw_t[:, :], b2s[:, :], start=True, stop=True)\
                      .then_inc(bias2, 1)

        @block.vector
        def _(dve):
            steps = Steps(vec_step)

            def step(instruction):
                dve.wait_ge(vec_step, steps.count(steps.after(instruction)))

            def rsqrt(mean, scale, eps, v, y, a, result):
                step(dve.tensor_scalar(v, mean, scale, eps, ALU.mult, ALU.add))
                step(dve.tensor_scalar(y.bitcast(I32), v.bitcast(I32), -0.5, RSQRT_SEED, ALU.mult, ALU.add))
                for last in (False, False, True):
                    step(dve.tensor_tensor(a, y, y, ALU.mult))
                    step(dve.scalar_tensor_tensor(out=a, in0=a, scalar=-0.5, in1=v, op0=ALU.mult, op1=ALU.mult))
                    step(dve.scalar_tensor_tensor(out=result if last else y, in0=a, scalar=1.5, in1=y,
                                                  op0=ALU.add, op1=ALU.mult))

            def layernorm_stats(src):
                step(dve.bn_stats(st6[:, :], src))
                step(dve.bn_aggr(mv[:, :], st6[:, :]))
                rsqrt(mv[:, 1:2], 1.0, LN_EPS, s_v[:, :], s_y[:, :], s_a[:, :], rstd[:, :])

            def layernorm(dst, src):
                layernorm_stats(src)
                return dve.tensor_scalar(dst, src, mv[:, 0:1], rstd[:, 0:1], ALU.subtract, ALU.mult)

            dve.wait_ge(x_in, 16)
            layernorm(xn[:, :], xs[:, :]).then_inc(ln_ready, 1)
            dve.wait_ge(cols_in, 16)
            dve.tensor_tensor(b_rz[:, :], colv[:, B_IH:B_IH + 2 * C], colv[:, B_HH:B_HH + 2 * C], ALU.add)
            dve.tensor_scalar(b_hn[:, :], colv[:, B_HH + 2 * C:B_HH + G], 0.5, None, ALU.mult)
            dve.wait_ge(x_t, 1)
            for b in range(B):
                src = bank[4][:, 0:C * T].rearrange("p (c k) -> p c k", c=C)[:, :, b * K:(b + 1) * K]
                dve.tensor_copy(slots[:, :, b * K:(b + 1) * K], src).then_inc(slots_ready[b], 1)

            for b in range(B):
                dve.wait_ge(ctx_in[b], 16)
                for t in range(0, MT, 2):
                    last = dve.tensor_tensor_reduce(squares_at(b, t), context_tile(b, t), context_tile(b, t), 1.0, 0.0,
                                                    ALU.mult, ALU.add, ms[:, b, t:t + 1])
                step(last)
                dve.wait_ge(ctx_sq, b + 1)
                rsqrt(ms[:, b, :], 1.0 / D, RMS_EPS, ms_v[:, :], ms_y[:, :], ms_a[:, :], ms_a[:, :])
                dve.tensor_copy(r_ctx[:, b, :], ms_a[:, :]).then_inc(r_ready, 1)
                dve.wait_ge(r_ready, b + 1)
                for t in range(0, MT, 2):
                    dve.tensor_scalar(ctx_n[:, b, t, :], ctx_n[:, b, t, :], r_ctx[:, b, t:t + 1], None,
                                      ALU.mult).then_inc(ctx_n_vec, 1)
                if b == 0:
                    dve.wait_ge(w_qk_done, 1)
                    dve.wait_ge(rows_in, 16)
                    for i in range(C):
                        last = dve.scalar_tensor_tensor(
                            out=w_qk[:, i, :], in0=bank[7][:, i * D:(i + 1) * D],
                            scalar=colv[:, W_SLOT + i:W_SLOT + i + 1], in1=rowv[:, R_IN:R_IN + D],
                            op0=ALU.mult, op1=ALU.mult)
                    last.then_inc(w_out, 1)
                for j in range(b * MT // 2 + 1, (b + 1) * MT // 2, 2):
                    dve.wait_ge(pair_t, j + 1)
                    src = bank[pair_banks[j % 3]][:, :].rearrange("p (c m) -> p c m", c=C)
                    dve.tensor_copy(ctx_t[:, :, j * 2 * P:(j + 1) * 2 * P], src).then_inc(pair_vec, 1)
                if b == 0:
                    dve.wait_ge(w_vi_done, 1)
                    for i in range(C):
                        w_in = colv[:, W_IN + i:W_IN + i + 1]
                        dve.tensor_scalar(w_vi[:, i, 0:2 * C * P], bank[2 + i][:, :], w_in, None, ALU.mult)
                        last = dve.tensor_scalar(w_vi[:, i, 2 * C * P:G * P], bank[5][:, i * C * P:(i + 1) * C * P],
                                                 w_in, None, ALU.mult)
                    last.then_inc(w_out, 1)

            def per_chunk(col, n):
                return col.unsqueeze(2).to_broadcast([P, n, K])

            def per_token(tile):
                return tile.unsqueeze(1).to_broadcast([P, C, K])

            def scale_query(b, turn):
                dve.wait_ge(q_raw[b], turn + 1)
                rsqrt(ssq_ps[b], 1.0 / D, RMS_EPS, rs_v[b][:, :], rs_y[b][:, :], rs_a[b][:, :], rs_a[b][:, :])
                dve.scalar_tensor_tensor(out=q_t[b][:, :, :], in0=q_ps[b], scalar=SCALE,
                                         in1=per_token(rs_a[b][:, :]), op0=ALU.mult, op1=ALU.mult)\
                   .then_inc(q_ready[b], 1)

            def shift_scores(b, turn):
                dve.wait_ge(scores_ready[b], turn + 1)
                step(dve.tensor_reduce(mx[b][:, :], scores[b], AX_X, ALU.max))
                dve.tensor_tensor(attn[b][:, :, :], scores[b], mx[b][:, :].unsqueeze(2).to_broadcast([P, MT, K]),
                                  ALU.subtract).then_inc(shifted[b], 1)

            def normalise(b, turn):
                dve.wait_ge(exp_ready[b], turn + 1)
                step(dve.tensor_reduce(den[b][:, :], attn[b][:, :, :], AX_X, ALU.add))
                step(dve.reciprocal(den[b][:, :], den[b][:, :]))
                dve.tensor_tensor(attn[b][:, :, :], attn[b][:, :, :],
                                  den[b][:, :].unsqueeze(2).to_broadcast([P, MT, K]), ALU.mult)\
                   .then_inc(attn_ready[b], 1)

            def hidden_n(b, turn):
                dve.wait_ge(gh_ready[b], turn + 1)
                step(dve.scalar_tensor_tensor(out=hh[b][:, :, :], in0=gates[b][:, HN:HN + C, :], scalar=0.5,
                                              in1=per_chunk(b_hn[:, :], C), op0=ALU.mult, op1=ALU.add))
                step(dve.tensor_tensor(hq[b][:, :, :], hh[b][:, :, :],
                                       per_chunk(colv[:, B_IH + 2 * C:B_IH + G], C), ALU.add))

            def scale_update(b, turn):
                dve.wait_ge(u_raw[b], turn + 1)
                step(dve.tensor_scalar(rs_v[b][:, :], sum_ps[b], SUM_EPS, None, ALU.add))
                step(dve.reciprocal(rs_y[b][:, :], rs_v[b][:, :]))
                dve.tensor_tensor(u_t[b][:, :, :], u_ps[b], per_token(rs_y[b][:, :]), ALU.mult)\
                   .then_inc(u_ready[b], 1)

            def gate(b, turn):
                dve.wait_ge(gx_ready[b], turn + 1)
                dve.tensor_tensor(rz[b][:, :, :], gates[b][:, 0:2 * C, :], per_chunk(b_rz[:, :], 2 * C), ALU.add)\
                   .then_inc(rz_pre[b], 1)
                step(dve.tensor_tensor(nn[b][:, :, :], gates[b][:, XN:XN + C, :], hq[b][:, :, :], ALU.add))
                dve.wait_ge(rz_ready[b], turn + 1)
                step(dve.tensor_tensor(n2[b][:, :, :], rz[b][:, 0:C, :], hh[b][:, :, :], ALU.mult))
                dve.tensor_tensor(nn[b][:, :, :], nn[b][:, :, :], n2[b][:, :, :], ALU.add).then_inc(n_pre[b], 1)
                mine = slots[:, :, b * K:(b + 1) * K]
                dve.wait_ge(n_ready[b], turn + 1)
                step(dve.tensor_tensor(n2[b][:, :, :], mine, nn[b][:, :, :], ALU.subtract))
                step(dve.scalar_tensor_tensor(out=n2[b][:, :, :], in0=rz[b][:, C:2 * C, :], scalar=1.0,
                                              in1=n2[b][:, :, :], op0=ALU.add, op1=ALU.mult))
                dve.scalar_tensor_tensor(out=mine, in0=n2[b][:, :, :], scalar=0.5, in1=nn[b][:, :, :],
                                         op0=ALU.mult, op1=ALU.add).then_inc(slots_ready[b], 1)

            with dve.Fori(0, TURNS) as turn:
                steps.enter(turn, STEPS_PER_TURN)
                scale_query(0, turn)
                scale_query(1, turn)
                shift_scores(0, turn)
                hidden_n(0, turn)
                normalise(0, turn)
                shift_scores(1, turn)
                hidden_n(1, turn)
                normalise(1, turn)
                scale_update(0, turn)
                gate(0, turn)
                scale_update(1, turn)
                gate(1, turn)
            steps.leave(TURNS)

            dve.wait_ge(slots_back, 1)
            step(dve.tensor_tensor(x1[:, :], bank[6][:, 0:D], xs[:, :], ALU.add))
            step(layernorm(xn[:, :], x1[:, :]))
            dve.tensor_reduce(red[:, :], xn[:, :].rearrange("p (h k) -> p k h", h=HEADS), AX_X, ALU.add)\
               .then_inc(red_ready, 1)
            dve.wait_ge(m_raw, 1)
            dve.tensor_scalar(m_t[:, :], bank[7][0:DK, 0:P], 1.0 / (B * HEADS), None, ALU.mult).then_inc(m_ready, 1)
            dve.wait_ge(ang_raw, 1)
            dve.tensor_scalar(ang[:, :], bank[7][:, P:2 * P], PI, -PI, ALU.min, ALU.max).then_inc(ang_ready, 1)
            dve.wait_ge(sin_ready, 1)
            dve.tensor_tensor(mixw[:, :], ang[:, :], ang[:, :], ALU.mult).then_inc(sin2_ready, 1)
            dve.wait_ge(consts_ready, CONSTS)
            dve.wait_ge(mix_exp, 1)
            dve.tensor_tensor_reduce(mixw[:, :], mixw[:, :], same_batch[:, :], 1.0, 0.0, ALU.mult, ALU.add,
                                     row_sum[:, :]).then_inc(mix_ready, 1)
            dve.wait_ge(mix_ready, 1)
            step(dve.reciprocal(row_inv[:, :], row_sum[:, :]))
            dve.wait_ge(mixed, 1)
            step(dve.scalar_tensor_tensor(out=x2[:, :], in0=bank[6][:, 0:D], scalar=row_inv[:, 0:1],
                                          in1=x1[:, :], op0=ALU.mult, op1=ALU.add))
            layernorm(xn[:, :], x2[:, :]).then_inc(ln_ready, 2)
            dve.wait_ge(x_t, 2)
            dve.tensor_copy(xf_t[:, :, :], bank[7][:, 0:C * T].rearrange("p (c k) -> p c k", c=C))\
               .then_inc(xf_ready, 1)

            dve.wait_ge(gate_raw, 1)
            step(dve.tensor_tensor(gl[:, :], bank[6][:, 0:E], rowv[:, R_BG:R_BG + E], ALU.add))
            dve.tensor_reduce(gneg[:, :], gl[:, :], AX_X, ALU.max, negate=True).then_inc(gate_ready, 1)
            dve.wait_ge(gate_exp, 1)
            step(dve.reciprocal(ginv[:, :], gsum[:, :]))
            step(dve.tensor_scalar(gl[:, :], gl[:, :], ginv[:, 0:1], None, ALU.mult))
            step(dve.max(g8[:, :], gl[:, :]))
            step(dve.max_index(gix[:, :], g8[:, :], gl[:, :]))
            step(dve.tensor_copy(gixf[:, :], gix[:, :]))
            step(dve.tensor_scalar(gtop[:, 0:1], g8[:, 0:1], g8[:, 1:2], GATE_EPS, ALU.add, ALU.add))
            step(dve.reciprocal(gtop[:, 1:2], gtop[:, 0:1]))
            step(dve.tensor_scalar(gtop[:, 2:4], g8[:, 0:2], gtop[:, 1:2], None, ALU.mult))
            for i in range(2):
                step(dve.tensor_scalar(pick[:, i, :], iota[:, :], gixf[:, i:i + 1], gtop[:, 2 + i:3 + i],
                                       ALU.is_equal, ALU.mult))
            dve.tensor_tensor(cw[:, :], pick[:, 0, :], pick[:, 1, :], ALU.add).then_inc(cw_ready, 1)
            dve.wait_ge(cw_turned, 1)
            dve.tensor_copy(cw_t[:, :], bank[7][0:E, 256:256 + P]).then_inc(cw_t_ready, 1)
            dve.wait_ge(bias2, 1)
            step(dve.tensor_copy(acc[:, :], bank[6][:, 256:256 + D]))
            dve.wait_ge(cw_ready, 1)
            for e in range(E):
                dve.wait_ge(down_done, FC * (e + 1))
                dve.scalar_tensor_tensor(out=acc[:, :], in0=bank[4 + e % 2][:, 0:D], scalar=cw[:, e:e + 1],
                                         in1=acc[:, :], op0=ALU.mult, op1=ALU.add).then_inc(y_folded, 1)
                dve.wait_ge(y_folded, e + 1)
            step(layernorm(acc[:, :], acc[:, :]))
            step(dve.tensor_tensor(acc[:, :], acc[:, :], rowv[:, R_GAMMA:R_GAMMA + D], ALU.mult))
            step(dve.tensor_tensor(x2[:, :], x2[:, :], rowv[:, R_BETA:R_BETA + D], ALU.add))
            dve.tensor_tensor(fin[:, :], acc[:, :], x2[:, :], ALU.add).then_inc(fin_ready, 1)


STEPS_PER_TURN = 44


def kernel(**inputs):
    import numpy as np
    import concourse.bacc as bacc
    from concourse.bass_utils import run_bass_kernel_spmd

    a = {k: np.asarray(v) for k, v in inputs.items()}
    B, K, D = a["x"].shape
    C = D // P
    E = a["L0_ffn_Wg"].shape[1]
    FF = a["L0_ffn_W1"].shape[2]

    def chunked(w):
        return w.reshape(-1, P, w.shape[-1]).transpose(1, 0, 2)

    def column(v):
        return v.reshape(-1, P).T

    x = a["x"].reshape(B * K, D)
    attn_w = np.stack([chunked(a[f"L0_xattn_W{n}"]) for n in "qkv"], axis=1)
    gru_w = np.stack([chunked(a[f"L0_xattn_gru_w{n}h"].T) for n in "ih"], axis=1)
    w1 = a["L0_ffn_W1"].reshape(E, C, P, FF).transpose(0, 2, 1, 3).reshape(E, P, C * FF)
    w2 = a["L0_ffn_W2"].reshape(E, FF // P, P, D).transpose(0, 2, 1, 3).reshape(E, P, C * FF)
    expert_w = np.concatenate([w1, w2], axis=2)
    cols = np.concatenate(
        [column(a["L0_xattn_slot_norm_w"]), column(a["L0_xattn_input_norm_w"]), column(a["L0_xattn_gru_bih"]),
         column(a["L0_xattn_gru_bhh"]), column(a["L0_ffn_b1"].reshape(-1)),
         chunked(a["L0_ffn_Wg"]).reshape(P, C * E)], axis=1)
    rows = np.concatenate([a["L0_xattn_input_norm_w"], a["L0_ffn_bg"], a["L0_ffn_gamma"], a["L0_ffn_beta"]])[None]
    arrays = {"in_x": x, "in_ctx": a["ctx_1024"], "in_attn_w": attn_w, "in_gru_w": gru_w,
              "in_expert_w": expert_w, "in_cols": cols, "in_rows": rows, "in_b2": a["L0_ffn_b2"]}
    arrays = {k: np.ascontiguousarray(v) for k, v in arrays.items()}

    nc = bacc.Bacc("TRN2", target_bir_lowering=False, num_devices=1)
    args = [nc.dram_tensor(n, v.shape, mybir.dt.from_np(v.dtype), kind="ExternalInput").ap()
            for n, v in arrays.items()]
    out = nc.dram_tensor("out", x.shape, F32, kind="ExternalOutput").ap()
    perceiver_layer(nc, *args, out)
    r = run_bass_kernel_spmd(nc, [arrays], core_ids=[0])
    return r.results[0]["out"].reshape(B, K, D)
```

```python
from contextlib import ExitStack

import concourse.bass as bass
from concourse import mybir

F32 = mybir.dt.float32
I32 = mybir.dt.int32
U32 = mybir.dt.uint32
ALU = mybir.AluOpType
ACT = mybir.ActivationFunctionType
AX_X = mybir.AxisListType.X

P = 128
RSQRT_SEED = 1597463007.0
PI = 3.1415927410125732


class Steps:

    def __init__(self, sem):
        self.sem, self.base, self.local, self.turn, self.per_turn = sem, 0, 0, None, 0

    def after(self, instruction):
        instruction.then_inc(self.sem, 1)
        self.local += 1
        return self.local

    def count(self, local):
        if self.turn is None:
            return self.base + local
        return self.turn * self.per_turn + (self.base + local)

    def enter(self, turn, per_turn):
        self.base, self.local, self.turn, self.per_turn = self.base + self.local, 0, turn, per_turn

    def leave(self, turns):
        assert self.local == self.per_turn, (self.local, self.per_turn)
        self.base, self.local, self.turn = self.base + turns * self.per_turn, 0, None


def perceiver_layer(nc, x, ctx, attn_w, gru_w, expert_w, cols, rows, b2, out):
    B, M, D = ctx.shape
    T = x.shape[0]
    K = T // B
    C = D // P
    E = expert_w.shape[0]
    MT = M // P
    FC = (expert_w.shape[2] // (2 * C)) // P
    FF = FC * P
    G = 3 * C
    TURNS = 3
    HEADS = 16
    DK = D // HEADS
    RMS_EPS, SUM_EPS, LN_EPS, GATE_EPS = 1e-6, 1e-6, 1e-5, 1e-8
    SCALE = float(D) ** -0.5
    assert T == P and B == 2 and C == 2

    W_SLOT, W_IN = 0, C
    B_IH = 2 * C
    B_HH = B_IH + G
    B1 = B_HH + G
    WG = B1 + E * FC
    NCOLS = WG + C * E
    R_IN, R_BG, R_GAMMA, R_BETA = 0, D, D + E, 2 * D + E
    NROWS = 3 * D + E
    assert cols.shape[1] == NCOLS and rows.shape[1] == NROWS

    with ExitStack() as stack:
        def sb(name, shape, dt=F32):
            return stack.enter_context(nc.sbuf_tensor(name, shape, dt))

        def sem(name):
            return stack.enter_context(nc.semaphore(name))

        bank = [None] * 8
        scores_ps = stack.enter_context(nc.psum_tensor("scores_ps", [P, B, MT, T], F32))
        gates_ps = stack.enter_context(nc.psum_tensor("gates_ps", [P, 4 * C, T], F32))
        for i in range(4):
            bank[i] = scores_ps[:, i // 2, (i % 2) * MT // 2:(i % 2 + 1) * MT // 2, :].rearrange("p t k -> p (t k)")
        for i in range(2):
            bank[4 + i] = gates_ps[:, i * 2 * C:(i + 1) * 2 * C, :].rearrange("p g k -> p (g k)")
        for i in (6, 7):
            bank[i] = stack.enter_context(nc.psum_tensor(f"bank{i}", [P, 512], F32))[:, :]

        def inside(area):
            at = [0]

            def place(shape):
                n = 1
                for k in shape[1:]:
                    n *= k
                assert at[0] + n <= area.shape[1]
                view = area[:, at[0]:at[0] + n]
                at[0] += n
                if len(shape) == 3:
                    view = view.rearrange("p (a b) -> p a b", a=shape[1])
                return view

            return place

        w1w2 = sb("w1w2", [P, E, 2 * C * FF])
        ctx_n = sb("ctx_n", [P, B, MT, D + 1])
        ctx_t = sb("ctx_t", [P, C, B * M])
        aw = sb("aw", [P, 3, C, D])
        gw = sb("gw", [P, 2, C, G * P])
        w_qk = sb("w_qk", [P, C, D])
        w_vi = sb("w_vi", [P, C, G * P])
        colv = sb("colv", [P, NCOLS])
        rowv = sb("rowv", [P, NROWS])
        b2s = sb("b2s", [E, D])
        xs = sb("xs", [P, D])
        xn = sb("xn", [P, D])
        ident = sb("ident", [P, P])
        ones = sb("ones", [P, P])
        same_batch = sb("same_batch", [P, P])
        same_slot = sb("same_slot", [P, P])
        slots = sb("slots", [P, C, T])
        attn = sb("attn", [P, B, MT, K])
        mx = sb("mx", [P, B, MT])
        den = sb("den", [P, B, MT])
        loop_tile = inside(aw[:, :, :, :].rearrange("p w c d -> p (w c d)"))
        sq = loop_tile([P, C, T])
        q_t = loop_tile([P, C, T])
        rz = loop_tile([P, 2 * C, T])
        hh = loop_tile([P, C, T])
        hq = loop_tile([P, C, T])
        nn = sb("nn", [P, C, T])
        zh = sb("zh", [P, C, T])
        u_n = sb("u_n", [P, D])
        u_t = sb("u_t", [P, C, T])
        rs_v = sb("rs_v", [P, T])
        rs_y = sb("rs_y", [P, T])
        rs_a = sb("rs_a", [P, T])
        c_v = sb("c_v", [P, 1])
        c_inv = sb("c_inv", [P, 1])
        b_rz = sb("b_rz", [P, 2 * C])
        b_hn = sb("b_hn", [P, C])
        ms = sb("ms", [P, B, MT])
        ms_v = sb("ms_v", [P, MT])
        ms_y = sb("ms_y", [P, MT])
        ms_a = sb("ms_a", [P, MT])
        r_ctx = sb("r_ctx", [P, B, MT])
        st6 = sb("st6", [P, 6])
        mv = sb("mv", [P, 2])
        s_v = sb("s_v", [P, 1])
        s_y = sb("s_y", [P, 1])
        s_a = sb("s_a", [P, 1])
        rstd = sb("rstd", [P, 1])
        later = inside(ctx_t[:, :, :].rearrange("p c m -> p (c m)"))

        x1 = later([P, D])
        red = later([P, DK])
        m_t = sb("m_t", [DK, P])
        ang = later([P, P])
        mixw = later([P, P])
        row_sum = sb("row_sum", [P, 1])
        row_inv = sb("row_inv", [P, 1])
        x2 = later([P, D])
        xf_t = later([P, C, T])
        gl = later([P, E])
        g8 = later([P, 8])
        gneg = later([P, 1])
        gsum = later([P, 1])
        ginv = later([P, 1])
        gtop = later([P, 8])
        gix = sb("gix", [P, 8], U32)
        gixf = later([P, 8])
        iota = sb("iota", [P, E])
        pick = later([P, 2, E])
        cw = later([P, E])
        cw_t = sb("cw_t", [E, P])
        h_t = later([P, 4, T])
        acc = later([P, D])
        fin = later([P, D])

        x_in, cols_in, rows_in, b2_in = sem("x_in"), sem("cols_in"), sem("rows_in"), sem("b2_in")
        aw_in, gw_in = sem("aw_in"), sem("gw_in")
        ctx_in = [sem(f"ctx_in{b}") for b in range(B)]
        expert_in = [sem(f"expert_in{e}") for e in range(E)]
        out_done = sem("out_done")
        pool_step, consts_ready = sem("pool_step"), sem("consts_ready")
        vec_step = sem("vec_step")
        ln_ready = sem("ln_ready")
        ctx_sq = sem("ctx_sq")
        r_ready = sem("r_ready")
        ctx_n_act, ctx_n_vec = sem("ctx_n_act"), sem("ctx_n_vec")
        pair_t = sem("pair_t")
        pair_act, pair_vec = sem("pair_act"), sem("pair_vec")
        x_t = sem("x_t")
        w_qk_done, w_vi_done = sem("w_qk_done"), sem("w_vi_done")
        w_out = sem("w_out")
        slots_ready = sem("slots_ready")
        sq_ready = sem("sq_ready")
        q_raw = sem("q_raw")
        gh_ready = sem("gh_ready")
        q_ready = sem("q_ready")
        scores_ready = sem("scores_ready")
        shifted = sem("shifted")
        exp_ready = sem("exp_ready")
        attn_ready = sem("attn_ready")
        u_raw = sem("u_raw")
        u_n_ready = sem("u_n_ready")
        u_turned = sem("u_turned")
        u_ready = sem("u_ready")
        gx_ready = sem("gx_ready")
        r_gate = sem("r_gate")
        z_gate = sem("z_gate")
        n_pre = sem("n_pre")
        n_ready = sem("n_ready")
        slots_back = sem("slots_back")
        red_ready, m_raw, m_ready, ang_raw = sem("red_ready"), sem("m_raw"), sem("m_ready"), sem("ang_raw")
        ang_ready, sin_ready, sin2_ready, mix_exp, mix_ready = (
            sem("ang_ready"), sem("sin_ready"), sem("sin2_ready"), sem("mix_exp"), sem("mix_ready"))
        mixed = sem("mixed")
        xf_ready = sem("xf_ready")
        gate_raw, gate_ready, gate_exp, cw_ready, cw_turned, cw_t_ready, bias2 = (
            sem("gate_raw"), sem("gate_ready"), sem("gate_exp"), sem("cw_ready"), sem("cw_turned"),
            sem("cw_t_ready"), sem("bias2"))
        hidden, gelu_done, down_done, y_ready, y_folded = (
            sem("hidden"), sem("gelu_done"), sem("down_done"), sem("y_ready"), sem("y_folded"))
        fin_ready = sem("fin_ready")

        q_ps = bank[6][:, 0:C * T].rearrange("p (c k) -> p c k", c=C)
        ssq_ps = bank[6][:, C * T:(C + 1) * T]
        u_ps = bank[7][:, 0:D + 1]
        GROUPS = 4
        GT = B * MT // GROUPS

        def group(tile, g):
            b, half = divmod(g, GROUPS // B)
            return tile[:, b, half * GT:(half + 1) * GT]

        pair_banks = [0, 1, 2]
        PAIRS = B * MT // 2
        HN, XN = 2 * C, 3 * C

        def context_tile(b, t):
            return ctx_n[:, b, t, 0:D].rearrange("p (c m) -> p c m", c=C)

        def squares_at(b, t):
            o = (b * MT + t) * P
            return ctx_t[:, :, o:o + P]

        def pair_act_count(j):
            return j // 2 + 1

        def pair_vec_count(j):
            return (j + 1) // 2

        block = stack.enter_context(nc.Block())

        @block.sync
        def _(sp):
            sp.dma_start(xs[:, :], x[:, :]).then_inc(x_in, 16)
            sp.dma_start(colv[:, :], cols[:, :]).then_inc(cols_in, 16)
            sp.dma_start(ctx_n[:, 0, :, 0:D], ctx[0].rearrange("(p t) d -> p t d", t=MT)).then_inc(ctx_in[0], 16)
            sp.dma_start(aw[:, :, :, :], attn_w[:, :, :, :]).then_inc(aw_in, 16)
            sp.dma_start(rowv[:, :], rows.to_broadcast([P, NROWS])).then_inc(rows_in, 16)
            sp.dma_start(ctx_n[:, 1, :, 0:D], ctx[1].rearrange("(p t) d -> p t d", t=MT)).then_inc(ctx_in[1], 16)
            sp.dma_start(gw[:, :, :, :], gru_w[:, :, :, :]).then_inc(gw_in, 16)
            sp.dma_start(b2s[:, :], b2[:, :]).then_inc(b2_in, 16)
            for e in range(E):
                sp.dma_start(w1w2[:, e, :], expert_w[e]).then_inc(expert_in[e], 16)
            sp.wait_ge(fin_ready, 1)
            sp.dma_start(out[:, :], fin[:, :]).then_inc(out_done, 16)
            sp.wait_ge(out_done, 16)

        @block.gpsimd
        def _(pool):
            def diagonal(m, base):
                return pool.affine_select(out=m[:, :], in_=m[:, :], compare_op=ALU.not_equal, fill=1.0,
                                          base=base, pattern=[[-1, P]], channel_multiplier=1)

            pool.memset(ident[:, :], 0.0).then_inc(pool_step, 1)
            pool.wait_ge(pool_step, 1)
            diagonal(ident, 0).then_inc(consts_ready, 1)
            pool.memset(ones[:, :], 1.0).then_inc(consts_ready, 1)
            pool.memset(ctx_n[:, :, :, D:D + 1], 1.0).then_inc(consts_ready, 1)
            pool.memset(same_batch[:, :], 0.0).then_inc(pool_step, 1)
            pool.memset(same_slot[:, :], 0.0).then_inc(pool_step, 1)
            pool.wait_ge(pool_step, 3)
            for b in range(B):
                pool.memset(same_batch[b * K:(b + 1) * K, b * K:(b + 1) * K], 1.0).then_inc(consts_ready, 1)
            pool.wait_ge(consts_ready, 3 + B)
            for i, base in enumerate((0, K, -K)):
                diagonal(same_slot, base).then_inc(pool_step, 1)
                pool.wait_ge(pool_step, 4 + i)
            pool.iota(iota[:, :], pattern=[[1, E]], base=0, channel_multiplier=0,
                      allow_small_or_imprecise_dtypes=True).then_inc(consts_ready, 1)

        CONSTS = 3 + B + 1

        @block.scalar
        def _(act):
            for b in range(B):
                act.wait_ge(ctx_in[b], 16)
                for t in range(1, MT, 2):
                    last = act.activation(squares_at(b, t), context_tile(b, t), ACT.Square,
                                          accum_out=ms[:, b, t:t + 1])
                last.then_inc(ctx_sq, 1)
                act.wait_ge(r_ready, b + 1)
                for t in range(1, MT, 2):
                    act.activation(ctx_n[:, b, t, 0:D], ctx_n[:, b, t, 0:D], ACT.Copy,
                                   scale=r_ctx[:, b, t:t + 1]).then_inc(ctx_n_act, 1)
                for j in range(b * MT // 2, (b + 1) * MT // 2, 2):
                    act.wait_ge(pair_t, j + 1)
                    src = bank[pair_banks[j % 3]].rearrange("p (c m) -> p c m", c=C)
                    act.activation(ctx_t[:, :, j * 2 * P:(j + 1) * 2 * P], src, ACT.Copy).then_inc(pair_act, 1)

            with act.Fori(0, TURNS) as turn:
                act.wait_ge(slots_ready, turn + 1)
                act.activation(sq[:, :, :], slots[:, :, :], ACT.Square).then_inc(sq_ready, 1)
                for g in range(GROUPS):
                    act.wait_ge(shifted, turn * GROUPS + (g + 1))
                    act.activation(group(attn, g), group(attn, g), ACT.Exp).then_inc(exp_ready, 1)
                act.wait_ge(gx_ready, turn * 3 + 1)
                for g in range(C):
                    last = act.activation(rz[:, g, :], gates_ps[:, g, :], ACT.Tanh, scale=0.5, bias=b_rz[:, g:g + 1])
                last.then_inc(r_gate, 1)
                act.wait_ge(gx_ready, turn * 3 + 3)
                for g in range(C, 2 * C):
                    last = act.activation(rz[:, g, :], gates_ps[:, g, :], ACT.Tanh, scale=0.5, bias=b_rz[:, g:g + 1])
                last.then_inc(z_gate, 1)
                act.wait_ge(n_pre, turn + 1)
                act.activation(nn[:, :, :], nn[:, :, :], ACT.Tanh).then_inc(n_ready, 1)

            act.wait_ge(ang_ready, 1)
            act.activation(ang[:, :], ang[:, :], ACT.Sin, scale=0.5).then_inc(sin_ready, 1)
            act.wait_ge(sin2_ready, 1)
            act.activation(mixw[:, :], mixw[:, :], ACT.Exp).then_inc(mix_exp, 1)
            act.wait_ge(gate_ready, 1)
            act.activation(gl[:, :], gl[:, :], ACT.Exp, bias=gneg[:, 0:1], accum_out=gsum[:, 0:1])\
               .then_inc(gate_exp, 1)
            for n in range(E * FC):
                act.wait_ge(hidden, n + 1)
                if n >= 4:
                    act.wait_ge(down_done, n - 3)
                act.activation(h_t[:, n % 4, :], bank[n % 4][:, 0:T], ACT.Gelu,
                               bias=colv[:, B1 + n:B1 + n + 1]).then_inc(gelu_done, 1)

        @block.tensor
        def _(pe):
            pe.wait_ge(consts_ready, 3)
            pe.wait_ge(ln_ready, 1)
            for c in range(C):
                last = pe.transpose(bank[6][:, c * T:(c + 1) * T], xn[:, c * P:(c + 1) * P], ident[:, :])
            last.then_inc(x_t, 1)
            pe.wait_ge(aw_in, 16)
            for i in range(C):
                for c in range(C):
                    last = pe.matmul(bank[7][:, i * D:(i + 1) * D], aw[:, 0, c, i * P:(i + 1) * P],
                                     aw[:, 1, c, :], start=(c == 0), stop=(c == C - 1))
            last.then_inc(w_qk_done, 1)

            def turn_pair(j):
                b, t = divmod(2 * j, MT)
                pe.wait_ge(ctx_n_vec, b * MT // 2 + t // 2 + 1)
                pe.wait_ge(ctx_n_act, b * MT // 2 + t // 2 + 1)
                if j >= 3:
                    if (j - 3) % 2:
                        pe.wait_ge(pair_vec, pair_vec_count(j - 3))
                    else:
                        pe.wait_ge(pair_act, pair_act_count(j - 3))
                for c in range(C):
                    for k in range(2):
                        o = (2 * c + k) * P
                        last = pe.transpose(bank[pair_banks[j % 3]][:, o:o + P],
                                            ctx_n[:, b, t + k, c * P:(c + 1) * P], ident[:, :])
                last.then_inc(pair_t, 1)

            for j in range(PAIRS // 2):
                turn_pair(j)
            pe.wait_ge(gw_in, 16)
            for i in range(C):
                for dst, g0, g1 in ((bank[4 + i], 0, 2 * C * P),
                                    (bank[3][:, i * C * P:(i + 1) * C * P], 2 * C * P, G * P)):
                    for c in range(C):
                        last = pe.matmul(dst, aw[:, 2, c, i * P:(i + 1) * P], gw[:, 0, c, g0:g1],
                                         start=(c == 0), stop=(c == C - 1))
            last.then_inc(w_vi_done, 1)
            for j in range(PAIRS // 2, PAIRS):
                turn_pair(j)
            pe.wait_ge(w_out, 2)
            pe.wait_ge(pair_act, PAIRS // 2)
            pe.wait_ge(pair_vec, PAIRS // 2)

            with pe.Fori(0, TURNS) as turn:
                pe.wait_ge(slots_ready, turn + 1)
                for i in range(C):
                    for c in range(C):
                        pe.matmul(q_ps[:, i, :], w_qk[:, c, i * P:(i + 1) * P], slots[:, c, :],
                                  start=(c == 0), stop=(c == C - 1))
                pe.wait_ge(sq_ready, turn + 1)
                for c in range(C):
                    last = pe.matmul(ssq_ps, ones[:, :], sq[:, c, :], start=(c == 0), stop=(c == C - 1))
                last.then_inc(q_raw, 1)
                for g in range(G):
                    for c in range(C):
                        last = pe.matmul(gates_ps[:, g, :], gw[:, 1, c, g * P:(g + 1) * P], slots[:, c, :],
                                         start=(g in (0, 2 * C) and c == 0), stop=False, skip_group_check=True)
                last.then_inc(gh_ready, 1)
                pe.wait_ge(q_ready, turn + 1)
                for g in range(GROUPS):
                    for k in range(GT):
                        b, t = divmod(g * GT + k, MT)
                        for c in range(C):
                            o = (b * MT + t) * P
                            last = pe.matmul(scores_ps[:, b, t, :], ctx_t[:, c, o:o + P], q_t[:, c, :],
                                             start=(c == 0), stop=(c == C - 1))
                    last.then_inc(scores_ready, 1)
                for g in range(GROUPS):
                    pe.wait_ge(attn_ready, turn * GROUPS + (g + 1))
                    for k in range(GT):
                        b, t = divmod(g * GT + k, MT)
                        last = pe.matmul(u_ps[b * K:(b + 1) * K, :], attn[:, b, t, :], ctx_n[:, b, t, :],
                                         start=(t == 0), stop=(t == MT - 1))
                last.then_inc(u_raw, 1)
                pe.wait_ge(u_n_ready, turn + 1)
                for c in range(C):
                    last = pe.transpose(q_ps[:, c, :], u_n[:, c * P:(c + 1) * P], ident[:, :])
                last.then_inc(u_turned, 1)
                pe.wait_ge(u_ready, turn + 1)
                for gate in (0, 2, 1):
                    if gate == 1:
                        pe.wait_ge(r_gate, turn + 1)
                    for i in range(C):
                        g = gate * C + i
                        dst = XN + i if gate == 2 else g
                        for c in range(C):
                            last = pe.matmul(gates_ps[:, dst, :], w_vi[:, c, g * P:(g + 1) * P], u_t[:, c, :],
                                             start=False, stop=(c == C - 1), skip_group_check=True)
                    last.then_inc(gx_ready, 1)

            pe.wait_ge(slots_ready, TURNS + 1)
            for c in range(C):
                last = pe.transpose(bank[6][:, c * P:(c + 1) * P], slots[:, c, :], ident[:, :])
            last.then_inc(slots_back, 1)
            pe.wait_ge(consts_ready, CONSTS)
            pe.wait_ge(red_ready, 1)
            pe.matmul(bank[7][0:DK, 0:P], red[:, :], same_slot[:, :], start=True, stop=True).then_inc(m_raw, 1)
            pe.wait_ge(m_ready, 1)
            pe.matmul(bank[7][:, P:2 * P], m_t[:, :], m_t[:, :], start=True, stop=True).then_inc(ang_raw, 1)
            pe.wait_ge(mix_ready, 1)
            pe.matmul(bank[6][:, 0:D], mixw[:, :], xn[:, :], start=True, stop=True).then_inc(mixed, 1)
            pe.wait_ge(ln_ready, 3)
            for c in range(C):
                last = pe.transpose(bank[7][:, c * T:(c + 1) * T], xn[:, c * P:(c + 1) * P], ident[:, :])
            last.then_inc(x_t, 1)
            pe.wait_ge(xf_ready, 1)
            for c in range(C):
                last = pe.matmul(bank[6][:, 0:E], xf_t[:, c, :], colv[:, WG + c * E:WG + (c + 1) * E],
                                 start=(c == 0), stop=(c == C - 1))
            last.then_inc(gate_raw, 1)

            def up(n):
                e, f = divmod(n, FC)
                if f == 0:
                    pe.wait_ge(expert_in[e], 16)
                if n >= 4:
                    pe.wait_ge(gelu_done, n - 3)
                for c in range(C):
                    last = pe.matmul(bank[n % 4][:, 0:T], w1w2[:, e, c * FF + f * P:c * FF + (f + 1) * P],
                                     xf_t[:, c, :], start=(c == 0), stop=(c == C - 1))
                last.then_inc(hidden, 1)

            def down(n):
                e, f = divmod(n, FC)
                pe.wait_ge(gelu_done, n + 1)
                if f == 0 and e >= 2:
                    pe.wait_ge(y_folded, e - 1)
                o = C * FF + f * D
                last = pe.matmul(bank[4 + e % 2][:, 0:D], h_t[:, n % 4, :], w1w2[:, e, o:o + D],
                                 start=(f == 0), stop=(f == FC - 1))
                last.then_inc(down_done, 1)

            LAG = 2
            for n in range(E * FC + LAG):
                if n < E * FC:
                    up(n)
                if n >= LAG:
                    down(n - LAG)
                if n == 6:
                    pe.wait_ge(cw_ready, 1)
                    pe.transpose(bank[7][0:E, 256:256 + P], cw[:, :], ident[:, :]).then_inc(cw_turned, 1)
                if n == 8:
                    pe.wait_ge(cw_t_ready, 1)
                    pe.wait_ge(b2_in, 16)
                    pe.matmul(bank[6][:, 256:256 + D], cw_t[:, :], b2s[:, :], start=True, stop=True)\
                      .then_inc(bias2, 1)

        @block.vector
        def _(dve):
            steps = Steps(vec_step)

            def step(instruction):
                dve.wait_ge(vec_step, steps.count(steps.after(instruction)))

            def rsqrt(mean, scale, eps, v, y, a, result):
                step(dve.tensor_scalar(v, mean, scale, eps, ALU.mult, ALU.add))
                step(dve.tensor_scalar(y.bitcast(I32), v.bitcast(I32), -0.5, RSQRT_SEED, ALU.mult, ALU.add))
                for last in (False, False, True):
                    step(dve.tensor_tensor(a, y, y, ALU.mult))
                    step(dve.scalar_tensor_tensor(out=a, in0=a, scalar=-0.5, in1=v, op0=ALU.mult, op1=ALU.mult))
                    step(dve.scalar_tensor_tensor(out=result if last else y, in0=a, scalar=1.5, in1=y,
                                                  op0=ALU.add, op1=ALU.mult))

            def layernorm_stats(src):
                step(dve.bn_stats(st6[:, :], src))
                step(dve.bn_aggr(mv[:, :], st6[:, :]))
                rsqrt(mv[:, 1:2], 1.0, LN_EPS, s_v[:, :], s_y[:, :], s_a[:, :], rstd[:, :])

            def layernorm(dst, src):
                layernorm_stats(src)
                return dve.tensor_scalar(dst, src, mv[:, 0:1], rstd[:, 0:1], ALU.subtract, ALU.mult)

            dve.wait_ge(x_in, 16)
            layernorm(xn[:, :], xs[:, :]).then_inc(ln_ready, 1)
            dve.wait_ge(cols_in, 16)
            step(dve.tensor_tensor(b_rz[:, :], colv[:, B_IH:B_IH + 2 * C], colv[:, B_HH:B_HH + 2 * C], ALU.add))
            dve.tensor_scalar(b_rz[:, :], b_rz[:, :], 0.5, None, ALU.mult)
            dve.tensor_scalar(b_hn[:, :], colv[:, B_HH + 2 * C:B_HH + G], 0.5, None, ALU.mult)
            dve.wait_ge(x_t, 1)
            dve.tensor_copy(slots[:, :, :], q_ps).then_inc(slots_ready, 1)

            for b in range(B):
                dve.wait_ge(ctx_in[b], 16)
                for t in range(0, MT, 2):
                    last = dve.tensor_tensor_reduce(squares_at(b, t), context_tile(b, t), context_tile(b, t), 1.0, 0.0,
                                                    ALU.mult, ALU.add, ms[:, b, t:t + 1])
                step(last)
                dve.wait_ge(ctx_sq, b + 1)
                rsqrt(ms[:, b, :], 1.0 / D, RMS_EPS, ms_v[:, :], ms_y[:, :], ms_a[:, :], ms_a[:, :])
                dve.tensor_copy(r_ctx[:, b, :], ms_a[:, :]).then_inc(r_ready, 1)
                dve.wait_ge(r_ready, b + 1)
                for t in range(0, MT, 2):
                    dve.tensor_scalar(ctx_n[:, b, t, 0:D], ctx_n[:, b, t, 0:D], r_ctx[:, b, t:t + 1], None,
                                      ALU.mult).then_inc(ctx_n_vec, 1)
                if b == 0:
                    dve.wait_ge(w_qk_done, 1)
                    dve.wait_ge(rows_in, 16)
                    for i in range(C):
                        last = dve.scalar_tensor_tensor(
                            out=w_qk[:, i, :], in0=bank[7][:, i * D:(i + 1) * D],
                            scalar=colv[:, W_SLOT + i:W_SLOT + i + 1], in1=rowv[:, R_IN:R_IN + D],
                            op0=ALU.mult, op1=ALU.mult)
                    last.then_inc(w_out, 1)
                for j in range(b * MT // 2 + 1, (b + 1) * MT // 2, 2):
                    dve.wait_ge(pair_t, j + 1)
                    src = bank[pair_banks[j % 3]].rearrange("p (c m) -> p c m", c=C)
                    dve.tensor_copy(ctx_t[:, :, j * 2 * P:(j + 1) * 2 * P], src).then_inc(pair_vec, 1)
                if b == 0:
                    dve.wait_ge(w_vi_done, 1)
                    for i in range(C):
                        w_in = colv[:, W_IN + i:W_IN + i + 1]
                        dve.tensor_scalar(w_vi[:, i, 0:2 * C * P], bank[4 + i], w_in, None, ALU.mult)
                        last = dve.tensor_scalar(w_vi[:, i, 2 * C * P:G * P], bank[3][:, i * C * P:(i + 1) * C * P],
                                                 w_in, None, ALU.mult)
                    last.then_inc(w_out, 1)

            def per_chunk(col):
                return col.unsqueeze(2).to_broadcast([P, C, T])

            def per_slot(tile):
                return tile.unsqueeze(2).to_broadcast([P, GT, K])

            def shift_scores(g, turn):
                b = g * GT // MT
                mine = group(scores_ps, g)[:, :, b * K:(b + 1) * K]
                dve.wait_ge(scores_ready, turn * GROUPS + (g + 1))
                step(dve.tensor_reduce(group(mx, g), mine, AX_X, ALU.max))
                dve.tensor_tensor(group(attn, g), mine, per_slot(group(mx, g)), ALU.subtract).then_inc(shifted, 1)

            def normalise(g, turn):
                dve.wait_ge(exp_ready, turn * GROUPS + (g + 1))
                step(dve.tensor_reduce(group(den, g), group(attn, g), AX_X, ALU.add))
                step(dve.reciprocal(group(den, g), group(den, g)))
                dve.tensor_tensor(group(attn, g), group(attn, g), per_slot(group(den, g)), ALU.mult)\
                   .then_inc(attn_ready, 1)

            with dve.Fori(0, TURNS) as turn:
                steps.enter(turn, STEPS_PER_TURN)
                dve.wait_ge(q_raw, turn + 1)
                rsqrt(ssq_ps, 1.0 / D, RMS_EPS, rs_v[:, :], rs_y[:, :], rs_a[:, :], rs_a[:, :])
                dve.scalar_tensor_tensor(out=q_t[:, :, :], in0=q_ps, scalar=SCALE,
                                         in1=rs_a[:, :].unsqueeze(1).to_broadcast([P, C, T]),
                                         op0=ALU.mult, op1=ALU.mult).then_inc(q_ready, 1)
                dve.wait_ge(gh_ready, turn + 1)
                step(dve.scalar_tensor_tensor(out=hh[:, :, :], in0=gates_ps[:, HN:HN + C, :], scalar=0.5,
                                              in1=per_chunk(b_hn[:, :]), op0=ALU.mult, op1=ALU.add))
                step(dve.tensor_tensor(hq[:, :, :], hh[:, :, :], per_chunk(colv[:, B_IH + 2 * C:B_IH + G]), ALU.add))
                for g in range(GROUPS):
                    shift_scores(g, turn)
                    if g >= 1:
                        normalise(g - 1, turn)
                normalise(GROUPS - 1, turn)
                dve.wait_ge(u_raw, turn + 1)
                step(dve.tensor_scalar(c_v[:, :], u_ps[:, D:D + 1], SUM_EPS, None, ALU.add))
                step(dve.reciprocal(c_inv[:, :], c_v[:, :]))
                dve.tensor_scalar(u_n[:, :], u_ps[:, 0:D], c_inv[:, 0:1], None, ALU.mult).then_inc(u_n_ready, 1)
                dve.wait_ge(u_turned, turn + 1)
                dve.tensor_copy(u_t[:, :, :], q_ps).then_inc(u_ready, 1)
                dve.wait_ge(r_gate, turn + 1)
                step(dve.tensor_tensor(zh[:, :, :], rz[:, 0:C, :], hh[:, :, :], ALU.mult))
                step(dve.tensor_tensor(hq[:, :, :], hq[:, :, :], zh[:, :, :], ALU.add))
                dve.wait_ge(gx_ready, turn * 3 + 2)
                dve.tensor_tensor(nn[:, :, :], gates_ps[:, XN:XN + C, :], hq[:, :, :], ALU.add).then_inc(n_pre, 1)
                dve.wait_ge(z_gate, turn + 1)
                step(dve.tensor_scalar(hh[:, :, :], rz[:, C:2 * C, :], 0.5, 0.5, ALU.mult, ALU.add))
                step(dve.tensor_tensor(zh[:, :, :], hh[:, :, :], slots[:, :, :], ALU.mult))
                step(dve.tensor_scalar(hh[:, :, :], hh[:, :, :], -1.0, 1.0, ALU.mult, ALU.add))
                dve.wait_ge(n_ready, turn + 1)
                step(dve.tensor_tensor(nn[:, :, :], nn[:, :, :], hh[:, :, :], ALU.mult))
                dve.tensor_tensor(slots[:, :, :], nn[:, :, :], zh[:, :, :], ALU.add).then_inc(slots_ready, 1)
            steps.leave(TURNS)

            dve.wait_ge(slots_back, 1)
            step(dve.tensor_tensor(x1[:, :], bank[6][:, 0:D], xs[:, :], ALU.add))
            step(layernorm(xn[:, :], x1[:, :]))
            dve.tensor_reduce(red[:, :], xn[:, :].rearrange("p (h k) -> p k h", h=HEADS), AX_X, ALU.add)\
               .then_inc(red_ready, 1)
            dve.wait_ge(m_raw, 1)
            dve.tensor_scalar(m_t[:, :], bank[7][0:DK, 0:P], 1.0 / (B * HEADS), None, ALU.mult).then_inc(m_ready, 1)
            dve.wait_ge(ang_raw, 1)
            dve.tensor_scalar(ang[:, :], bank[7][:, P:2 * P], PI, -PI, ALU.min, ALU.max).then_inc(ang_ready, 1)
            dve.wait_ge(sin_ready, 1)
            dve.tensor_tensor(mixw[:, :], ang[:, :], ang[:, :], ALU.mult).then_inc(sin2_ready, 1)
            dve.wait_ge(consts_ready, CONSTS)
            dve.wait_ge(mix_exp, 1)
            dve.tensor_tensor_reduce(mixw[:, :], mixw[:, :], same_batch[:, :], 1.0, 0.0, ALU.mult, ALU.add,
                                     row_sum[:, :]).then_inc(mix_ready, 1)
            dve.wait_ge(mix_ready, 1)
            step(dve.reciprocal(row_inv[:, :], row_sum[:, :]))
            dve.wait_ge(mixed, 1)
            step(dve.scalar_tensor_tensor(out=x2[:, :], in0=bank[6][:, 0:D], scalar=row_inv[:, 0:1],
                                          in1=x1[:, :], op0=ALU.mult, op1=ALU.add))
            layernorm(xn[:, :], x2[:, :]).then_inc(ln_ready, 2)
            dve.wait_ge(x_t, 2)
            dve.tensor_copy(xf_t[:, :, :], bank[7][:, 0:C * T].rearrange("p (c k) -> p c k", c=C))\
               .then_inc(xf_ready, 1)

            dve.wait_ge(gate_raw, 1)
            step(dve.tensor_tensor(gl[:, :], bank[6][:, 0:E], rowv[:, R_BG:R_BG + E], ALU.add))
            dve.tensor_reduce(gneg[:, :], gl[:, :], AX_X, ALU.max, negate=True).then_inc(gate_ready, 1)
            dve.wait_ge(gate_exp, 1)
            step(dve.reciprocal(ginv[:, :], gsum[:, :]))
            step(dve.tensor_scalar(gl[:, :], gl[:, :], ginv[:, 0:1], None, ALU.mult))
            step(dve.max(g8[:, :], gl[:, :]))
            step(dve.max_index(gix[:, :], g8[:, :], gl[:, :]))
            step(dve.tensor_copy(gixf[:, :], gix[:, :]))
            step(dve.tensor_scalar(gtop[:, 0:1], g8[:, 0:1], g8[:, 1:2], GATE_EPS, ALU.add, ALU.add))
            step(dve.reciprocal(gtop[:, 1:2], gtop[:, 0:1]))
            step(dve.tensor_scalar(gtop[:, 2:4], g8[:, 0:2], gtop[:, 1:2], None, ALU.mult))
            for i in range(2):
                step(dve.tensor_scalar(pick[:, i, :], iota[:, :], gixf[:, i:i + 1], gtop[:, 2 + i:3 + i],
                                       ALU.is_equal, ALU.mult))
            dve.tensor_tensor(cw[:, :], pick[:, 0, :], pick[:, 1, :], ALU.add).then_inc(cw_ready, 1)
            dve.wait_ge(cw_turned, 1)
            dve.tensor_copy(cw_t[:, :], bank[7][0:E, 256:256 + P]).then_inc(cw_t_ready, 1)
            dve.wait_ge(bias2, 1)
            step(dve.tensor_copy(acc[:, :], bank[6][:, 256:256 + D]))
            dve.wait_ge(cw_ready, 1)
            for e in range(E):
                dve.wait_ge(down_done, FC * (e + 1))
                dve.scalar_tensor_tensor(out=acc[:, :], in0=bank[4 + e % 2][:, 0:D], scalar=cw[:, e:e + 1],
                                         in1=acc[:, :], op0=ALU.mult, op1=ALU.add).then_inc(y_folded, 1)
                dve.wait_ge(y_folded, e + 1)
            step(layernorm(acc[:, :], acc[:, :]))
            step(dve.tensor_tensor(acc[:, :], acc[:, :], rowv[:, R_GAMMA:R_GAMMA + D], ALU.mult))
            step(dve.tensor_tensor(x2[:, :], x2[:, :], rowv[:, R_BETA:R_BETA + D], ALU.add))
            dve.tensor_tensor(fin[:, :], acc[:, :], x2[:, :], ALU.add).then_inc(fin_ready, 1)


STEPS_PER_TURN = 33


def kernel(**inputs):
    import numpy as np
    import concourse.bacc as bacc
    from concourse.bass_utils import run_bass_kernel_spmd

    a = {k: np.asarray(v) for k, v in inputs.items()}
    B, K, D = a["x"].shape
    C = D // P
    E = a["L0_ffn_Wg"].shape[1]
    FF = a["L0_ffn_W1"].shape[2]

    def chunked(w):
        return w.reshape(-1, P, w.shape[-1]).transpose(1, 0, 2)

    def column(v):
        return v.reshape(-1, P).T

    x = a["x"].reshape(B * K, D)
    attn_w = np.stack([chunked(a[f"L0_xattn_W{n}"]) for n in "qkv"], axis=1)
    gru_w = np.stack([chunked(a[f"L0_xattn_gru_w{n}h"].T) for n in "ih"], axis=1)
    w1 = a["L0_ffn_W1"].reshape(E, C, P, FF).transpose(0, 2, 1, 3).reshape(E, P, C * FF)
    w2 = a["L0_ffn_W2"].reshape(E, FF // P, P, D).transpose(0, 2, 1, 3).reshape(E, P, C * FF)
    expert_w = np.concatenate([w1, w2], axis=2)
    cols = np.concatenate(
        [column(a["L0_xattn_slot_norm_w"]), column(a["L0_xattn_input_norm_w"]), column(a["L0_xattn_gru_bih"]),
         column(a["L0_xattn_gru_bhh"]), column(a["L0_ffn_b1"].reshape(-1)),
         chunked(a["L0_ffn_Wg"]).reshape(P, C * E)], axis=1)
    rows = np.concatenate([a["L0_xattn_input_norm_w"], a["L0_ffn_bg"], a["L0_ffn_gamma"], a["L0_ffn_beta"]])[None]
    arrays = {"in_x": x, "in_ctx": a["ctx_1024"], "in_attn_w": attn_w, "in_gru_w": gru_w,
              "in_expert_w": expert_w, "in_cols": cols, "in_rows": rows, "in_b2": a["L0_ffn_b2"]}
    arrays = {k: np.ascontiguousarray(v) for k, v in arrays.items()}

    nc = bacc.Bacc("TRN2", target_bir_lowering=False, num_devices=1)
    args = [nc.dram_tensor(n, v.shape, mybir.dt.from_np(v.dtype), kind="ExternalInput").ap()
            for n, v in arrays.items()]
    out = nc.dram_tensor("out", x.shape, F32, kind="ExternalOutput").ap()
    perceiver_layer(nc, *args, out)
    r = run_bass_kernel_spmd(nc, [arrays], core_ids=[0])
    return r.results[0]["out"].reshape(B, K, D)
```

```python
from contextlib import ExitStack

import concourse.bass as bass
from concourse import mybir

F32 = mybir.dt.float32
U32 = mybir.dt.uint32
ALU = mybir.AluOpType
ACT = mybir.ActivationFunctionType
AX_X = mybir.AxisListType.X

P = 128
PI = 3.1415927410125732


class Steps:

    def __init__(self, sem):
        self.sem, self.base, self.local, self.turn, self.per_turn = sem, 0, 0, None, 0

    def after(self, instruction):
        instruction.then_inc(self.sem, 1)
        self.local += 1
        return self.local

    def count(self, local):
        if self.turn is None:
            return self.base + local
        return self.turn * self.per_turn + (self.base + local)

    def enter(self, turn, per_turn):
        self.base, self.local, self.turn, self.per_turn = self.base + self.local, 0, turn, per_turn

    def leave(self, turns):
        assert self.local == self.per_turn, (self.local, self.per_turn)
        self.base, self.local, self.turn = self.base + turns * self.per_turn, 0, None


def perceiver_layer(nc, x, ctx, attn_w, gru_w, expert_w, cols, rows, b2, out):
    B, M, D = ctx.shape
    T = x.shape[0]
    K = T // B
    C = D // P
    E = expert_w.shape[0]
    MT = M // P
    FC = (expert_w.shape[2] // (2 * C)) // P
    FF = FC * P
    G = 3 * C
    TURNS = 3
    HEADS = 16
    DK = D // HEADS
    RMS_EPS, SUM_EPS, LN_EPS, GATE_EPS = 1e-6, 1e-6, 1e-5, 1e-8
    SCALE = float(D) ** -0.5
    assert T == P and B == 2 and C == 2 and MT == 8

    W_SLOT, W_IN = 0, C
    B_IH = 2 * C
    B_HH = B_IH + G
    B1 = B_HH + G
    WG = B1 + E * FC
    NCOLS = WG + C * E
    R_BG, R_GAMMA, R_BETA = 0, E, D + E
    NROWS = 2 * D + E
    assert cols.shape[1] == NCOLS and rows.shape[1] == NROWS

    with ExitStack() as stack:
        def sb(name, shape, dt=F32):
            return stack.enter_context(nc.sbuf_tensor(name, shape, dt))

        def sem(name):
            return stack.enter_context(nc.semaphore(name))

        bank = [None] * 8
        scores_ps = stack.enter_context(nc.psum_tensor("scores_ps", [P, MT, B, T], F32))
        gates_ps = stack.enter_context(nc.psum_tensor("gates_ps", [P, 4 * C, T], F32))
        for i in range(4):
            bank[i] = scores_ps[:, i * MT // 4:(i + 1) * MT // 4, :, :].rearrange("p t b k -> p (t b k)")
        for i in range(2):
            bank[4 + i] = gates_ps[:, i * 2 * C:(i + 1) * 2 * C, :].rearrange("p g k -> p (g k)")
        for i in (6, 7):
            bank[i] = stack.enter_context(nc.psum_tensor(f"bank{i}", [P, 512], F32))[:, :]

        def inside(area):
            at = [0]

            def place(shape):
                n = 1
                for k in shape[1:]:
                    n *= k
                assert at[0] + n <= area.shape[1]
                view = area[:, at[0]:at[0] + n]
                at[0] += n
                if len(shape) == 3:
                    view = view.rearrange("p (a b) -> p a b", a=shape[1])
                return view

            return place

        w1w2 = sb("w1w2", [P, E, 2 * C * FF])
        ctx_n = sb("ctx_n", [P, B, MT, D + 1])
        ctx_t = sb("ctx_t", [P, C, B * M])
        aw = sb("aw", [P, 3, C, D])
        gw = sb("gw", [P, 2, C, G * P])
        w_qk = sb("w_qk", [P, C, D])
        w_vi = sb("w_vi", [P, C, G * P])
        colv = sb("colv", [P, NCOLS])
        rowv = sb("rowv", [P, NROWS])
        b2s = sb("b2s", [E, D])
        xs = sb("xs", [P, D])
        xn = sb("xn", [P, D])
        ident = sb("ident", [P, P])
        ones = sb("ones", [P, P])
        same_slot = sb("same_slot", [P, P])
        slots = sb("slots", [P, C, T])
        attn = sb("attn", [P, MT, B, K])
        s_copy = sb("s_copy", [P, 2, MT // 4 * P])
        neg_max = sb("neg_max", [P, MT, B])
        den = sb("den", [P, MT, B])
        loop_tile = inside(aw[:, :, :, :].rearrange("p w c d -> p (w c d)"))
        sq = loop_tile([P, C, T])
        q_t = loop_tile([P, C, T])
        rz = loop_tile([P, 2 * C, T])
        hh = loop_tile([P, C, T])
        half_slots = loop_tile([P, C, T])
        rh = sb("rh", [P, C, T])
        nn = sb("nn", [P, C, T])
        u_n = sb("u_n", [P, D])
        u_t = sb("u_t", [P, C, T])
        rms = sb("rms", [P, 1])
        rrms = sb("rrms", [P, 1])
        c_inv = sb("c_inv", [P, 1])
        b_rz = sb("b_rz", [P, 2 * C])
        b_hn = sb("b_hn", [P, C])
        ms = sb("ms", [P, B, MT])
        rms_ctx = sb("rms_ctx", [P, B, MT])
        r_ctx = sb("r_ctx", [P, B, MT])
        st6 = sb("st6", [P, 6])
        mv = sb("mv", [P, 2])
        dev = sb("dev", [P, 1])
        eps = sb("eps", [P, 3])
        rstd = sb("rstd", [P, 1])
        later = inside(ctx_t[:, :, :].rearrange("p c m -> p (c m)"))

        x1 = later([P, D])
        red = later([P, DK])
        mean_h = later([P, 1])
        m_t = sb("m_t", [DK, P])
        ang = later([P, K])
        mixw = later([P, K])
        row_sum = sb("row_sum", [P, 1])
        row_inv = sb("row_inv", [P, 1])
        x2 = later([P, D])
        xf_t = later([P, C, T])
        gl = later([P, E])
        g8 = later([P, 8])
        gneg = later([P, 1])
        gsum = later([P, 1])
        ginv = later([P, 1])
        gtop = later([P, 8])
        gix = sb("gix", [P, 8], U32)
        gixf = later([P, 8])
        iota = sb("iota", [P, E])
        pick = later([P, 2, E])
        cw = later([P, E])
        cw_t = sb("cw_t", [E, P])
        h_t = later([P, 4, T])
        acc = later([P, D])
        fin = later([P, D])

        x_in, cols_in, rows_in, b2_in = sem("x_in"), sem("cols_in"), sem("rows_in"), sem("b2_in")
        wqk_in, wv_in, wih_in, whh_in = sem("wqk_in"), sem("wv_in"), sem("wih_in"), sem("whh_in")
        ctx_in = [[sem(f"ctx_in{b}_{h}") for h in range(2)] for b in range(B)]
        expert_in = [sem(f"expert_in{e}") for e in range(E)]
        out_done = sem("out_done")
        pool_step, consts_ready = sem("pool_step"), sem("consts_ready")
        vec_step = sem("vec_step")
        ln_ready = sem("ln_ready")
        eps_ready = sem("eps_ready")
        var_ready = sem("var_ready")
        dev_ready = sem("dev_ready")
        x1_ready = sem("x1_ready")
        x1n_ready = sem("x1n_ready")
        ctx_sq = sem("ctx_sq")
        ctx_sq_vec = sem("ctx_sq_vec")
        ctx_rms = sem("ctx_rms")
        r_ready = sem("r_ready")
        ctx_n_act, ctx_n_vec = sem("ctx_n_act"), sem("ctx_n_vec")
        pair_t = sem("pair_t")
        pair_act, pair_vec = sem("pair_act"), sem("pair_vec")
        x_t = sem("x_t")
        w_qk_done, w_vi_done = sem("w_qk_done"), sem("w_vi_done")
        w_qk_out = sem("w_qk_out")
        w_vi_vec, w_vi_act = sem("w_vi_vec"), sem("w_vi_act")
        slots_ready = sem("slots_ready")
        sq_ready = sem("sq_ready")
        ssq_ready = sem("ssq_ready")
        rms_ready = sem("rms_ready")
        q_raw = sem("q_raw")
        gh_ready = sem("gh_ready")
        hh_ready = sem("hh_ready")
        q_ready = sem("q_ready")
        s_rows_ready = sem("s_rows_ready")
        s_copied = sem("s_copied")
        scores_ready = sem("scores_ready")
        max_ready = sem("max_ready")
        exp_ready = sem("exp_ready")
        attn_ready = sem("attn_ready")
        u_raw = sem("u_raw")
        u_n_ready = sem("u_n_ready")
        u_turned = sem("u_turned")
        u_ready = sem("u_ready")
        r_done, z_done = sem("r_done"), sem("z_done")
        xn_done = sem("xn_done")
        r_gate = sem("r_gate")
        z_gate = sem("z_gate")
        n_pre = sem("n_pre")
        n_ready = sem("n_ready")
        slots_back = sem("slots_back")
        red_ready, m_raw, m_ready, ang_raw = sem("red_ready"), sem("m_raw"), sem("m_ready"), sem("ang_raw")
        ang_ready, sin_ready, sin2_ready, mix_exp = (
            sem("ang_ready"), sem("sin_ready"), sem("sin2_ready"), sem("mix_exp"))
        mixed = sem("mixed")
        xf_ready = sem("xf_ready")
        gate_raw, gate_ready, gate_exp, cw_ready, cw_turned, cw_t_ready, bias2 = (
            sem("gate_raw"), sem("gate_ready"), sem("gate_exp"), sem("cw_ready"), sem("cw_turned"),
            sem("cw_t_ready"), sem("bias2"))
        hidden, gelu_done = sem("hidden"), sem("gelu_done")
        down_done = sem("down_done")
        y_folded = sem("y_folded")
        fin_ready = sem("fin_ready")

        r_ps = bank[6][:, 0:C * T].rearrange("p (c k) -> p c k", c=C)
        q_ps = bank[6][:, C * T:2 * C * T].rearrange("p (c k) -> p c k", c=C)
        z_ps = gates_ps[:, 0:C, :]
        hn_ps = gates_ps[:, 2 * C:3 * C, :]
        xn_ps = [gates_ps[:, 3 * C, :], q_ps[:, 0, :]]
        u_ps = bank[7][:, 0:D + 1]
        ut_ps = [bank[3 - c][:, 0:T] for c in range(C)]
        ssq_ps = bank[7][:, 511:512]
        xf_ps = [bank[7][:, 0:T], bank[4][:, 0:T]]
        gate_ps = bank[5][:, 0:E]
        GROUPS = 4
        GT = MT // GROUPS

        def group(tile, g):
            return tile[:, g * GT:(g + 1) * GT]

        def s_rows(g):
            return bank[g % 2][:, 0:GT * P]

        def s_turned(g):
            return bank[(2 + g) % 4][:, 0:GT * T].rearrange("p (t b k) -> p t b k", t=GT, b=B)

        pair_banks = [4, 5, 7]
        PAIRS = B * MT // 2

        def context_tile(b, t):
            return ctx_n[:, b, t, 0:D].rearrange("p (c m) -> p c m", c=C)

        def squares_at(b, t):
            o = (b * MT + t) * P
            return ctx_t[:, :, o:o + P]

        def pair_act_count(j):
            return j // 2 + 1

        def pair_vec_count(j):
            return (j + 1) // 2

        def combined(i):
            return ((bank[2 * i], slice(0, 512)), (bank[2 * i + 1][:, 0:G * P - 512], slice(512, G * P)))

        block = stack.enter_context(nc.Block())

        @block.sync
        def _(sp):
            sp.dma_start(xs[:, :], x[:, :]).then_inc(x_in, 16)
            sp.dma_start(colv[:, :], cols[:, :]).then_inc(cols_in, 16)
            sp.dma_start(aw[:, 0:2, :, :], attn_w[:, 0:2, :, :]).then_inc(wqk_in, 16)

            def load_context(b):
                src = ctx[b].rearrange("(p t) d -> p t d", t=MT)
                for h in range(2):
                    part = slice(h * MT // 2, (h + 1) * MT // 2)
                    sp.dma_start(ctx_n[:, b, part, 0:D], src[:, part, :]).then_inc(ctx_in[b][h], 16)

            load_context(0)
            sp.dma_start(aw[:, 2, :, :], attn_w[:, 2, :, :]).then_inc(wv_in, 16)
            sp.dma_start(gw[:, 0, :, :], gru_w[:, 0, :, :]).then_inc(wih_in, 16)
            load_context(1)
            sp.dma_start(gw[:, 1, :, :], gru_w[:, 1, :, :]).then_inc(whh_in, 16)
            sp.dma_start(rowv[:, :], rows.to_broadcast([P, NROWS])).then_inc(rows_in, 16)
            sp.dma_start(b2s[:, :], b2[:, :]).then_inc(b2_in, 16)
            for e in range(E):
                sp.dma_start(w1w2[:, e, :], expert_w[e]).then_inc(expert_in[e], 16)
            sp.wait_ge(fin_ready, 1)
            sp.dma_start(out[:, :], fin[:, :]).then_inc(out_done, 16)
            sp.wait_ge(out_done, 16)

        @block.gpsimd
        def _(pool):
            def diagonal(m, base):
                return pool.affine_select(out=m[:, :], in_=m[:, :], compare_op=ALU.not_equal, fill=1.0,
                                          base=base, pattern=[[-1, P]], channel_multiplier=1)

            pool.memset(eps[:, 0:1], RMS_EPS).then_inc(eps_ready, 1)
            pool.memset(eps[:, 1:2], LN_EPS).then_inc(eps_ready, 1)
            pool.memset(eps[:, 2:3], SUM_EPS / P).then_inc(eps_ready, 1)
            pool.memset(ident[:, :], 0.0).then_inc(pool_step, 1)
            pool.wait_ge(pool_step, 1)
            diagonal(ident, 0).then_inc(consts_ready, 1)
            pool.memset(ones[:, :], 1.0).then_inc(consts_ready, 1)
            pool.memset(ctx_n[:, :, :, D:D + 1], 1.0).then_inc(consts_ready, 1)
            pool.memset(same_slot[:, :], 0.0).then_inc(pool_step, 1)
            pool.wait_ge(pool_step, 2)
            for i, base in enumerate((0, K, -K)):
                diagonal(same_slot, base).then_inc(pool_step, 1)
                pool.wait_ge(pool_step, 3 + i)
            pool.iota(iota[:, :], pattern=[[1, E]], base=0, channel_multiplier=0,
                      allow_small_or_imprecise_dtypes=True).then_inc(consts_ready, 1)

        CONSTS = 4

        @block.scalar
        def _(act):
            def context_squares(b):
                for t in range(1, MT, 2):
                    act.wait_ge(ctx_in[b][t * 2 // MT], 16)
                    last = act.activation(squares_at(b, t), context_tile(b, t), ACT.Square,
                                          accum_out=ms[:, b, t:t + 1])
                last.then_inc(ctx_sq, 1)

            def context_scale(b):
                act.wait_ge(ctx_sq, b + 1)
                act.wait_ge(ctx_sq_vec, b + 1)
                act.activation(rms_ctx[:, b, :], ms[:, b, :], ACT.Sqrt, scale=1.0 / D, bias=eps[:, 0:1])\
                   .then_inc(ctx_rms, 1)
                act.wait_ge(r_ready, b + 1)
                for t in range(1, MT, 2):
                    act.activation(ctx_n[:, b, t, 0:D], ctx_n[:, b, t, 0:D], ACT.Copy,
                                   scale=r_ctx[:, b, t:t + 1]).then_inc(ctx_n_act, 1)

            def copy_pairs(b):
                for j in range(b * MT // 2, (b + 1) * MT // 2, 2):
                    act.wait_ge(pair_t, j + 1)
                    src = bank[pair_banks[j % 3]].rearrange("p (c m) -> p c m", c=C)
                    act.activation(ctx_t[:, :, j * 2 * P:(j + 1) * 2 * P], src, ACT.Copy).then_inc(pair_act, 1)

            def deviation(n):
                act.wait_ge(var_ready, n)
                act.activation(dev[:, :], mv[:, 1:2], ACT.Sqrt, bias=eps[:, 1:2]).then_inc(dev_ready, 1)

            act.wait_ge(eps_ready, 3)
            deviation(1)
            context_squares(0)
            context_scale(0)
            copy_pairs(0)
            context_squares(1)
            context_scale(1)
            act.wait_ge(w_vi_done, 1)
            act.wait_ge(cols_in, 16)
            for src, cols_of in combined(0):
                last = act.activation(w_vi[:, 0, cols_of], src, ACT.Copy, scale=colv[:, W_IN:W_IN + 1])
            last.then_inc(w_vi_act, 1)
            copy_pairs(1)

            def slots_rms(turn):
                act.wait_ge(ssq_ready, turn + 1)
                act.activation(rms[:, :], ssq_ps, ACT.Sqrt, scale=1.0 / D, bias=eps[:, 0:1]).then_inc(rms_ready, 1)

            def softmax_and_gates(turn):
                for g in range(GROUPS):
                    act.wait_ge(max_ready, turn * GROUPS + (g + 1))
                    for t in range(g * GT, (g + 1) * GT):
                        for b in range(B):
                            last = act.activation(attn[:, t, b, :], s_turned(g)[:, t - g * GT, b, :], ACT.Exp,
                                                  bias=neg_max[:, t, b:b + 1], accum_out=den[:, t, b:b + 1])
                        last.then_inc(exp_ready, 1)
                act.wait_ge(r_done, turn + 1)
                for c in range(C):
                    last = act.activation(rz[:, c, :], r_ps[:, c, :], ACT.Tanh, scale=0.5, bias=b_rz[:, c:c + 1])
                last.then_inc(r_gate, 1)
                act.wait_ge(z_done, turn + 1)
                for c in range(C):
                    act.activation(rz[:, C + c, :], z_ps[:, c, :], ACT.Tanh, scale=0.5,
                                   bias=b_rz[:, C + c:C + c + 1]).then_inc(z_gate, 1)
                for c in range(C):
                    act.wait_ge(n_pre, turn * C + (c + 1))
                    act.activation(nn[:, c, :], nn[:, c, :], ACT.Tanh,
                                   bias=colv[:, B_IH + 2 * C + c:B_IH + 2 * C + c + 1]).then_inc(n_ready, 1)

            slots_rms(0)
            with act.Fori(0, TURNS - 1) as turn:
                softmax_and_gates(turn)
                slots_rms(turn + 1)
            softmax_and_gates(TURNS - 1)
            deviation(2)
            act.wait_ge(ang_ready, 1)
            act.activation(ang[:, :], ang[:, :], ACT.Sin, scale=0.5).then_inc(sin_ready, 1)
            act.wait_ge(sin2_ready, 1)
            act.activation(mixw[:, :], mixw[:, :], ACT.Exp, accum_out=row_sum[:, 0:1]).then_inc(mix_exp, 1)
            deviation(3)
            act.wait_ge(gate_ready, 1)
            act.activation(gl[:, :], gate_ps, ACT.Exp, bias=gneg[:, 0:1], accum_out=gsum[:, 0:1])\
               .then_inc(gate_exp, 1)
            for n in range(E * FC):
                act.wait_ge(hidden, n + 1)
                if n >= 4:
                    act.wait_ge(down_done, n - 3)
                act.activation(h_t[:, n % 4, :], bank[n % 4][:, 0:T], ACT.Gelu,
                               bias=colv[:, B1 + n:B1 + n + 1]).then_inc(gelu_done, 1)
            deviation(4)

        @block.tensor
        def _(pe):
            pe.wait_ge(eps_ready, 3)
            pe.wait_ge(consts_ready, 3)
            pe.wait_ge(ln_ready, 1)
            for c in range(C):
                last = pe.transpose(q_ps[:, c, :], xn[:, c * P:(c + 1) * P], ident[:, :])
            last.then_inc(x_t, 1)
            pe.wait_ge(wqk_in, 16)
            for i in range(C):
                for c in range(C):
                    last = pe.matmul(bank[3][:, i * D:(i + 1) * D], aw[:, 0, c, i * P:(i + 1) * P],
                                     aw[:, 1, c, :], start=(c == 0), stop=(c == C - 1))
            last.then_inc(w_qk_done, 1)

            def turn_pair(j):
                b, t = divmod(2 * j, MT)
                pe.wait_ge(ctx_n_vec, b * MT // 2 + t // 2 + 1)
                pe.wait_ge(ctx_n_act, b * MT // 2 + t // 2 + 1)
                if j >= 3:
                    if (j - 3) % 2:
                        pe.wait_ge(pair_vec, pair_vec_count(j - 3))
                    else:
                        pe.wait_ge(pair_act, pair_act_count(j - 3))
                for c in range(C):
                    for k in range(2):
                        o = (2 * c + k) * P
                        last = pe.transpose(bank[pair_banks[j % 3]][:, o:o + P],
                                            ctx_n[:, b, t + k, c * P:(c + 1) * P], ident[:, :])
                last.then_inc(pair_t, 1)

            def combine(i):
                for dst, cols_of in combined(i):
                    for c in range(C):
                        last = pe.matmul(dst, aw[:, 2, c, i * P:(i + 1) * P], gw[:, 0, c, cols_of],
                                         start=(c == 0), stop=(c == C - 1))
                last.then_inc(w_vi_done, 1)

            for j in range(PAIRS // 2):
                turn_pair(j)
            pe.wait_ge(wv_in, 16)
            pe.wait_ge(wih_in, 16)
            combine(0)
            pe.wait_ge(w_qk_out, 1)
            combine(1)
            for j in range(PAIRS // 2, PAIRS):
                turn_pair(j)
            pe.wait_ge(whh_in, 16)

            with pe.Fori(0, TURNS) as turn:
                def hidden_gate(gate, dst, c):
                    for i in range(C):
                        g = gate * C + i
                        last = pe.matmul(dst[:, i, :], gw[:, 1, c, g * P:(g + 1) * P], slots[:, c, :],
                                         start=(i == 0 and c == 0), stop=False, skip_group_check=True)
                    return last

                pe.wait_ge(w_qk_out, 1)
                for c in range(C):
                    pe.wait_ge(slots_ready, turn * C + (c + 1))
                    for i in range(C):
                        last = pe.matmul(q_ps[:, i, :], w_qk[:, c, i * P:(i + 1) * P], slots[:, c, :],
                                         start=(c == 0 and i == 0), stop=(c == C - 1), skip_group_check=True)
                last.then_inc(q_raw, 1)
                pe.wait_ge(pair_act, PAIRS // 2)
                pe.wait_ge(pair_vec, PAIRS // 2)
                for c in range(C):
                    hidden_gate(1, z_ps, c)
                pe.wait_ge(sq_ready, turn + 1)
                for c in range(C):
                    last = pe.matmul(ssq_ps, sq[:, c, :], ones[:, 0:1], start=(c == 0), stop=(c == C - 1))
                last.then_inc(ssq_ready, 1)
                pe.wait_ge(w_vi_act, 1)
                pe.wait_ge(w_vi_vec, 1)

                def score(g):
                    if g >= 2:
                        pe.wait_ge(s_copied, turn * GROUPS + (g - 1))
                    for c in range(C):
                        if g == 0:
                            pe.wait_ge(q_ready, turn * C + (c + 1))
                        for b in range(B):
                            o = (b * MT + g * GT) * P
                            last = pe.matmul(s_rows(g)[b * K:(b + 1) * K, :], q_t[:, c, b * K:(b + 1) * K],
                                             ctx_t[:, c, o:o + GT * P], start=(c == 0), stop=(c == C - 1),
                                             skip_group_check=True)
                    last.then_inc(s_rows_ready, 1)

                def turn_scores(g):
                    pe.wait_ge(s_copied, turn * GROUPS + (g + 1))
                    for t in range(GT):
                        last = pe.transpose(bank[(2 + g) % 4][:, t * T:(t + 1) * T],
                                            s_copy[:, g % 2, t * P:(t + 1) * P], ident[:, :])
                    last.then_inc(scores_ready, 1)

                def update(g):
                    for t in range(g * GT, (g + 1) * GT):
                        pe.wait_ge(attn_ready, turn * MT + (t + 1))
                        for b in range(B):
                            last = pe.matmul(u_ps[b * K:(b + 1) * K, :], attn[:, t, b, :], ctx_n[:, b, t, :],
                                             start=(t == 0), stop=(t == MT - 1), skip_group_check=True)
                        if t == 0:
                            pe.matmul(u_ps[:, D:D + 1], ones[:, :], eps[:, 2:3], start=False, stop=False,
                                      skip_group_check=True)
                    return last

                score(0)
                score(1)
                turn_scores(0)
                score(2)
                turn_scores(1)
                score(3)
                turn_scores(2)
                update(0)
                turn_scores(3)
                update(1)
                update(2)
                update(3).then_inc(u_raw, 1)
                for c in range(C):
                    last = hidden_gate(2, hn_ps, c)
                last.then_inc(gh_ready, 1)
                for c in range(C):
                    pe.wait_ge(u_n_ready, turn * C + (c + 1))
                    pe.transpose(ut_ps[c], u_n[:, c * P:(c + 1) * P], ident[:, :]).then_inc(u_turned, 1)
                for c in range(C):
                    hidden_gate(0, r_ps, c)
                def input_gate(i, dst, c, **flags):
                    return pe.matmul(dst, w_vi[:, c, i * P:(i + 1) * P], u_t[:, c, :],
                                     stop=(c == C - 1), skip_group_check=True, **flags)

                for c in range(C):
                    pe.wait_ge(u_ready, turn * C + (c + 1))
                    for i in range(C):
                        last = input_gate(i, r_ps[:, i, :], c, start=False)
                last.then_inc(r_done, 1)
                for i in range(C):
                    for c in range(C):
                        last = input_gate(C + i, z_ps[:, i, :], c, start=False)
                last.then_inc(z_done, 1)
                pe.wait_ge(hh_ready, turn + 1)
                for i in range(C):
                    if i == 1:
                        pe.wait_ge(r_gate, turn + 1)
                    for c in range(C):
                        last = input_gate(2 * C + i, xn_ps[i], c, start=(i == 1 and c == 0))
                    last.then_inc(xn_done, 1)

            for c in range(C):
                pe.matmul(bank[0][:, c * P:(c + 1) * P], ident[:, :], xs[:, c * P:(c + 1) * P],
                          start=(c == 0), stop=False, skip_group_check=True)
            for c in range(C):
                pe.wait_ge(slots_ready, TURNS * C + (c + 1))
                last = pe.matmul(bank[0][:, c * P:(c + 1) * P], slots[:, c, :], ident[:, :], start=False,
                                 stop=True, skip_group_check=True)
            last.then_inc(slots_back, 1)
            pe.wait_ge(consts_ready, CONSTS)
            pe.wait_ge(red_ready, 1)
            pe.matmul(bank[7][0:DK, 0:P], red[:, :], same_slot[:, :], start=True, stop=True).then_inc(m_raw, 1)
            pe.wait_ge(m_ready, 1)
            pe.matmul(bank[7][:, P:P + K], m_t[:, :], m_t[:, 0:K], start=True, stop=True).then_inc(ang_raw, 1)
            pe.wait_ge(x1n_ready, 1)
            pe.wait_ge(mix_exp, 1)
            for b in range(B):
                own = slice(b * K, (b + 1) * K)
                last = pe.matmul(bank[6][own, 0:D], mixw[own, :], xn[own, :], start=True, stop=True)
            last.then_inc(mixed, 1)
            pe.wait_ge(rows_in, 16)
            pe.matmul(gate_ps, ident[:, :], rowv[:, R_BG:R_BG + E], start=True, stop=False,
                      skip_group_check=True)
            for c in range(C):
                pe.wait_ge(ln_ready, c + 2)
                pe.transpose(xf_ps[c], xn[:, c * P:(c + 1) * P], ident[:, :]).then_inc(x_t, 1)
            for c in range(C):
                pe.wait_ge(xf_ready, c + 1)
                last = pe.matmul(gate_ps, xf_t[:, c, :], colv[:, WG + c * E:WG + (c + 1) * E],
                                 start=False, stop=(c == C - 1), skip_group_check=True)
            last.then_inc(gate_raw, 1)

            def up(n):
                e, f = divmod(n, FC)
                if f == 0:
                    pe.wait_ge(expert_in[e], 16)
                if n >= 4:
                    pe.wait_ge(gelu_done, n - 3)
                for c in range(C):
                    last = pe.matmul(bank[n % 4][:, 0:T], w1w2[:, e, c * FF + f * P:c * FF + (f + 1) * P],
                                     xf_t[:, c, :], start=(c == 0), stop=(c == C - 1))
                last.then_inc(hidden, 1)

            def down(n):
                e, f = divmod(n, FC)
                pe.wait_ge(gelu_done, n + 1)
                if f == 0 and e >= 2:
                    pe.wait_ge(y_folded, e - 1)
                o = C * FF + f * D
                last = pe.matmul(bank[4 + e % 2][:, 0:D], h_t[:, n % 4, :], w1w2[:, e, o:o + D],
                                 start=(f == 0), stop=(f == FC - 1))
                last.then_inc(down_done, 1)

            LAG = 3
            for n in range(E * FC + LAG):
                if n < E * FC:
                    up(n)
                if n >= LAG:
                    down(n - LAG)
                if n == 6:
                    pe.wait_ge(cw_ready, 1)
                    pe.transpose(bank[7][0:E, 256:256 + P], cw[:, :], ident[:, :]).then_inc(cw_turned, 1)
                if n == 8:
                    pe.wait_ge(cw_t_ready, 1)
                    pe.wait_ge(b2_in, 16)
                    pe.matmul(bank[6][:, 256:256 + D], cw_t[:, :], b2s[:, :], start=True, stop=True)\
                      .then_inc(bias2, 1)

        @block.vector
        def _(dve):
            steps = Steps(vec_step)

            def step(instruction):
                dve.wait_ge(vec_step, steps.count(steps.after(instruction)))

            def layernorm_stats(src):
                step(dve.bn_stats(st6[:, :], src))
                dve.bn_aggr(mv[:, :], st6[:, :]).then_inc(var_ready, 1)

            def layernorm_scale(n):
                dve.wait_ge(dev_ready, n)
                step(dve.reciprocal(rstd[:, :], dev[:, :]))

            def layernorm(dst, src):
                return dve.tensor_scalar(dst, src, mv[:, 0:1], rstd[:, 0:1], ALU.subtract, ALU.mult)

            dve.wait_ge(x_in, 16)
            layernorm_stats(xs[:, :])
            layernorm_scale(1)
            layernorm(xn[:, :], xs[:, :]).then_inc(ln_ready, 1)
            dve.wait_ge(cols_in, 16)
            step(dve.tensor_tensor(b_rz[:, :], colv[:, B_IH:B_IH + 2 * C], colv[:, B_HH:B_HH + 2 * C], ALU.add))
            dve.tensor_scalar(b_rz[:, :], b_rz[:, :], 0.5, None, ALU.mult)
            dve.tensor_scalar(b_hn[:, :], colv[:, B_HH + 2 * C:B_HH + G], 0.5, None, ALU.mult)
            dve.wait_ge(x_t, 1)
            dve.tensor_copy(slots[:, :, :], q_ps).then_inc(slots_ready, C)

            def context_squares(b):
                for t in range(0, MT, 2):
                    dve.wait_ge(ctx_in[b][t * 2 // MT], 16)
                    last = dve.tensor_tensor_reduce(squares_at(b, t), context_tile(b, t), context_tile(b, t), 1.0, 0.0,
                                                    ALU.mult, ALU.add, ms[:, b, t:t + 1])
                last.then_inc(ctx_sq_vec, 1)

            def context_scale(b):
                dve.wait_ge(ctx_rms, b + 1)
                dve.reciprocal(r_ctx[:, b, :], rms_ctx[:, b, :]).then_inc(r_ready, 1)
                dve.wait_ge(r_ready, b + 1)
                for t in range(0, MT, 2):
                    dve.tensor_scalar(ctx_n[:, b, t, 0:D], ctx_n[:, b, t, 0:D], r_ctx[:, b, t:t + 1], None,
                                      ALU.mult).then_inc(ctx_n_vec, 1)

            def copy_pairs(b):
                for j in range(b * MT // 2 + 1, (b + 1) * MT // 2, 2):
                    dve.wait_ge(pair_t, j + 1)
                    src = bank[pair_banks[j % 3]].rearrange("p (c m) -> p c m", c=C)
                    dve.tensor_copy(ctx_t[:, :, j * 2 * P:(j + 1) * 2 * P], src).then_inc(pair_vec, 1)

            context_squares(0)
            context_scale(0)
            copy_pairs(0)
            dve.wait_ge(w_qk_done, 1)
            for i in range(C):
                last = dve.tensor_scalar(w_qk[:, i, :], bank[3][:, i * D:(i + 1) * D],
                                         colv[:, W_SLOT + i:W_SLOT + i + 1], SCALE, ALU.mult, ALU.mult)
            last.then_inc(w_qk_out, 1)
            context_squares(1)
            context_scale(1)

            def square_slots():
                dve.tensor_tensor(sq[:, :, :], slots[:, :, :], slots[:, :, :], ALU.mult).then_inc(sq_ready, 1)

            dve.wait_ge(w_vi_done, C)
            dve.wait_ge(slots_ready, C)
            square_slots()
            copy_pairs(1)
            for src, cols_of in combined(1):
                last = dve.tensor_scalar(w_vi[:, 1, cols_of], src, colv[:, W_IN + 1:W_IN + 2], None, ALU.mult)
            last.then_inc(w_vi_vec, 1)

            def per_chunk(col):
                return col.unsqueeze(2).to_broadcast([P, C, T])

            with dve.Fori(0, TURNS) as turn:
                steps.enter(turn, STEPS_PER_TURN)
                dve.wait_ge(slots_ready, (turn + 1) * C)
                half = steps.after(dve.tensor_scalar(half_slots[:, :, :], slots[:, :, :], 0.5, None, ALU.mult))
                dve.wait_ge(q_raw, turn + 1)
                for c in range(C):
                    dve.tensor_scalar(q_t[:, c, :], q_ps[:, c, :], colv[:, W_IN + c:W_IN + c + 1], None,
                                      ALU.mult).then_inc(q_ready, 1)
                dve.wait_ge(rms_ready, turn + 1)
                step(dve.reciprocal(rrms[:, :], rms[:, :]))

                def maximum(g):
                    dve.wait_ge(scores_ready, turn * GROUPS + (g + 1))
                    dve.tensor_reduce(group(neg_max, g), s_turned(g), AX_X, ALU.max, negate=True)\
                       .then_inc(max_ready, 1)

                def normalise(g):
                    for t in range(g * GT, (g + 1) * GT):
                        dve.wait_ge(exp_ready, turn * MT + (t + 1))
                        step(dve.reciprocal(den[:, t, :], den[:, t, :]))
                        dve.tensor_tensor(attn[:, t, :, :], attn[:, t, :, :],
                                          den[:, t, :].unsqueeze(2).to_broadcast([P, B, K]), ALU.mult)\
                           .then_inc(attn_ready, 1)

                def copy_scores(g):
                    dve.wait_ge(s_rows_ready, turn * GROUPS + (g + 1))
                    if g >= 2:
                        dve.wait_ge(scores_ready, turn * GROUPS + (g - 1))
                    dve.tensor_scalar(s_copy[:, g % 2, :], s_rows(g), rrms[:, 0:1], None, ALU.mult)\
                       .then_inc(s_copied, 1)

                copy_scores(0)
                copy_scores(1)
                maximum(0)
                copy_scores(2)
                maximum(1)
                normalise(0)
                maximum(2)
                copy_scores(3)
                normalise(1)
                maximum(3)
                normalise(2)
                normalise(3)
                dve.wait_ge(u_raw, turn + 1)
                step(dve.reciprocal(c_inv[:, :], u_ps[:, D:D + 1]))
                for c in range(C):
                    dve.tensor_scalar(u_n[:, c * P:(c + 1) * P], u_ps[:, c * P:(c + 1) * P], c_inv[:, 0:1], None,
                                      ALU.mult).then_inc(u_n_ready, 1)
                for c in range(C):
                    dve.wait_ge(u_turned, turn * C + (c + 1))
                    dve.tensor_copy(u_t[:, c, :], ut_ps[c]).then_inc(u_ready, 1)
                dve.wait_ge(gh_ready, turn + 1)
                dve.scalar_tensor_tensor(out=hh[:, :, :], in0=hn_ps, scalar=0.5, in1=per_chunk(b_hn[:, :]),
                                         op0=ALU.mult, op1=ALU.add).then_inc(hh_ready, 1)
                dve.wait_ge(hh_ready, turn + 1)
                dve.wait_ge(r_gate, turn + 1)
                step(dve.scalar_tensor_tensor(out=rh[:, :, :], in0=rz[:, 0:C, :], scalar=1.0, in1=hh[:, :, :],
                                              op0=ALU.add, op1=ALU.mult))
                dve.wait_ge(vec_step, steps.count(half))
                kept = []
                for c in range(C):
                    dve.wait_ge(xn_done, turn * C + (c + 1))
                    dve.tensor_tensor(nn[:, c, :], xn_ps[c], rh[:, c, :], ALU.add).then_inc(n_pre, 1)
                    dve.wait_ge(z_gate, turn * C + (c + 1))
                    kept.append(steps.after(dve.scalar_tensor_tensor(
                        out=half_slots[:, c, :], in0=rz[:, C + c, :], scalar=1.0, in1=half_slots[:, c, :],
                        op0=ALU.add, op1=ALU.mult)))
                parts = []
                for c in range(C):
                    dve.wait_ge(n_ready, turn * C + (c + 1))
                    parts.append(steps.after(dve.scalar_tensor_tensor(
                        out=hh[:, c, :], in0=rz[:, C + c, :], scalar=1.0, in1=nn[:, c, :],
                        op0=ALU.subtract, op1=ALU.mult)))
                for c in range(C):
                    dve.wait_ge(vec_step, steps.count(max(kept[c], parts[c])))
                    dve.scalar_tensor_tensor(out=slots[:, c, :], in0=hh[:, c, :], scalar=-0.5,
                                             in1=half_slots[:, c, :], op0=ALU.mult, op1=ALU.add)\
                       .then_inc(slots_ready, 1)
                dve.wait_ge(slots_ready, (turn + 2) * C)
                square_slots()
            steps.leave(TURNS)

            dve.wait_ge(slots_back, 1)
            x1_ps = bank[0][:, 0:D]
            layernorm_stats(x1_ps)
            dve.wait_ge(var_ready, 2)
            step(dve.tensor_scalar(mean_h[:, :], mv[:, 0:1], float(HEADS), None, ALU.mult))
            step(dve.tensor_reduce(red[:, :], x1_ps.rearrange("p (h k) -> p k h", h=HEADS), AX_X, ALU.add))
            layernorm_scale(2)
            dve.tensor_scalar(red[:, :], red[:, :], mean_h[:, 0:1], rstd[:, 0:1], ALU.subtract, ALU.mult)\
               .then_inc(red_ready, 1)
            layernorm(xn[:, :], x1_ps).then_inc(x1n_ready, 1)
            dve.wait_ge(m_raw, 1)
            dve.tensor_scalar(m_t[:, :], bank[7][0:DK, 0:P], 1.0 / (B * HEADS), None, ALU.mult).then_inc(m_ready, 1)
            dve.wait_ge(ang_raw, 1)
            dve.tensor_scalar(ang[:, :], bank[7][:, P:P + K], PI, -PI, ALU.min, ALU.max).then_inc(ang_ready, 1)
            dve.tensor_copy(x1[:, :], x1_ps).then_inc(x1_ready, 1)
            dve.wait_ge(sin_ready, 1)
            dve.tensor_tensor(mixw[:, :], ang[:, :], ang[:, :], ALU.mult).then_inc(sin2_ready, 1)
            dve.wait_ge(mix_exp, 1)
            step(dve.reciprocal(row_inv[:, :], row_sum[:, :]))
            dve.wait_ge(x1_ready, 1)
            dve.wait_ge(mixed, 1)
            step(dve.scalar_tensor_tensor(out=x2[:, :], in0=bank[6][:, 0:D], scalar=row_inv[:, 0:1],
                                          in1=x1[:, :], op0=ALU.mult, op1=ALU.add))
            layernorm_stats(x2[:, :])
            layernorm_scale(3)
            for c in range(C):
                chunk = slice(c * P, (c + 1) * P)
                layernorm(xn[:, chunk], x2[:, chunk]).then_inc(ln_ready, 1)
            for c in range(C):
                dve.wait_ge(x_t, c + 2)
                dve.tensor_copy(xf_t[:, c, :], xf_ps[c]).then_inc(xf_ready, 1)

            dve.wait_ge(gate_raw, 1)
            dve.tensor_reduce(gneg[:, :], gate_ps, AX_X, ALU.max, negate=True).then_inc(gate_ready, 1)
            dve.wait_ge(gate_exp, 1)
            step(dve.reciprocal(ginv[:, :], gsum[:, :]))
            step(dve.tensor_scalar(gl[:, :], gl[:, :], ginv[:, 0:1], None, ALU.mult))
            step(dve.max(g8[:, :], gl[:, :]))
            step(dve.max_index(gix[:, :], g8[:, :], gl[:, :]))
            step(dve.tensor_copy(gixf[:, :], gix[:, :]))
            step(dve.tensor_scalar(gtop[:, 0:1], g8[:, 0:1], g8[:, 1:2], GATE_EPS, ALU.add, ALU.add))
            step(dve.reciprocal(gtop[:, 1:2], gtop[:, 0:1]))
            step(dve.tensor_scalar(gtop[:, 2:4], g8[:, 0:2], gtop[:, 1:2], None, ALU.mult))
            for i in range(2):
                step(dve.tensor_scalar(pick[:, i, :], iota[:, :], gixf[:, i:i + 1], gtop[:, 2 + i:3 + i],
                                       ALU.is_equal, ALU.mult))
            dve.tensor_tensor(cw[:, :], pick[:, 0, :], pick[:, 1, :], ALU.add).then_inc(cw_ready, 1)
            dve.wait_ge(cw_turned, 1)
            dve.tensor_copy(cw_t[:, :], bank[7][0:E, 256:256 + P]).then_inc(cw_t_ready, 1)
            dve.wait_ge(rows_in, 16)
            dve.wait_ge(bias2, 1)
            dve.tensor_tensor(x2[:, :], x2[:, :], rowv[:, R_BETA:R_BETA + D], ALU.add)
            step(dve.tensor_copy(acc[:, :], bank[6][:, 256:256 + D]))
            dve.wait_ge(cw_ready, 1)
            for e in range(E):
                dve.wait_ge(down_done, FC * (e + 1))
                dve.scalar_tensor_tensor(out=acc[:, :], in0=bank[4 + e % 2][:, 0:D], scalar=cw[:, e:e + 1],
                                         in1=acc[:, :], op0=ALU.mult, op1=ALU.add).then_inc(y_folded, 1)
                dve.wait_ge(y_folded, e + 1)
            layernorm_stats(acc[:, :])
            dve.wait_ge(var_ready, 4)
            dve.scalar_tensor_tensor(out=acc[:, :], in0=acc[:, :], scalar=mv[:, 0:1], in1=rowv[:, R_GAMMA:R_GAMMA + D],
                                     op0=ALU.subtract, op1=ALU.mult)
            layernorm_scale(4)
            dve.scalar_tensor_tensor(out=fin[:, :], in0=acc[:, :], scalar=rstd[:, 0:1], in1=x2[:, :],
                                     op0=ALU.mult, op1=ALU.add).then_inc(fin_ready, 1)


STEPS_PER_TURN = 16


def kernel(**inputs):
    import numpy as np
    import concourse.bacc as bacc
    from concourse.bass_utils import run_bass_kernel_spmd

    a = {k: np.asarray(v) for k, v in inputs.items()}
    B, K, D = a["x"].shape
    C = D // P
    E = a["L0_ffn_Wg"].shape[1]
    FF = a["L0_ffn_W1"].shape[2]

    def chunked(w):
        return w.reshape(-1, P, w.shape[-1]).transpose(1, 0, 2)

    def column(v):
        return v.reshape(-1, P).T

    x = a["x"].reshape(B * K, D)
    attn_w = np.stack([chunked(a[f"L0_xattn_W{n}"]) for n in "qkv"], axis=1)
    gru_w = np.stack([chunked(a[f"L0_xattn_gru_w{n}h"].T) for n in "ih"], axis=1)
    w1 = a["L0_ffn_W1"].reshape(E, C, P, FF).transpose(0, 2, 1, 3).reshape(E, P, C * FF)
    w2 = a["L0_ffn_W2"].reshape(E, FF // P, P, D).transpose(0, 2, 1, 3).reshape(E, P, C * FF)
    expert_w = np.concatenate([w1, w2], axis=2)
    cols = np.concatenate(
        [column(a["L0_xattn_slot_norm_w"]), column(a["L0_xattn_input_norm_w"]), column(a["L0_xattn_gru_bih"]),
         column(a["L0_xattn_gru_bhh"]), column(a["L0_ffn_b1"].reshape(-1)),
         chunked(a["L0_ffn_Wg"]).reshape(P, C * E)], axis=1)
    rows = np.concatenate([a["L0_ffn_bg"], a["L0_ffn_gamma"], a["L0_ffn_beta"]])[None]
    arrays = {"in_x": x, "in_ctx": a["ctx_1024"], "in_attn_w": attn_w, "in_gru_w": gru_w,
              "in_expert_w": expert_w, "in_cols": cols, "in_rows": rows, "in_b2": a["L0_ffn_b2"]}
    arrays = {k: np.ascontiguousarray(v) for k, v in arrays.items()}

    nc = bacc.Bacc("TRN2", target_bir_lowering=False, num_devices=1)
    args = [nc.dram_tensor(n, v.shape, mybir.dt.from_np(v.dtype), kind="ExternalInput").ap()
            for n, v in arrays.items()]
    out = nc.dram_tensor("out", x.shape, F32, kind="ExternalOutput").ap()
    perceiver_layer(nc, *args, out)
    r = run_bass_kernel_spmd(nc, [arrays], core_ids=[0])
    return r.results[0]["out"].reshape(B, K, D)
```
